# Optimizing a Trainium2 kernel written in Bass

```python
import numpy as np
import jax
import jax.numpy as jnp

def _softmax(x, axis=-1):
    return jax.nn.softmax(x, axis=axis)

def _gelu(x):
    return jax.nn.gelu(x, approximate=True)

def _silu(x):
    return jax.nn.silu(x)

def _sigmoid(x):
    return jax.nn.sigmoid(x)

def _layernorm(x, axis=-1, eps=1e-05):
    m = jnp.mean(x, axis=axis, keepdims=True)
    v = jnp.var(x, axis=axis, keepdims=True)
    return (x - m) / jnp.sqrt(v + eps)

def _scatter_add(tgt, idx, src, axis=0):
    return tgt.at[idx].add(src)

def _segment_sum(src, seg, n):
    return jax.ops.segment_sum(src, seg, n)
kernel_name = 'mk_xattn_ffn_d1_seqx_r8_6848a2'

def setup_inputs(seed: int=0):
    np.random.seed(seed)
    _w = jnp.asarray

    def _rec_inputs():
        import jax
        import jax.numpy as jnp
        _rk = jax.random.key(seed)
        x = 4.136e-05 + 0.9999 * jax.random.normal(jax.random.fold_in(_rk, 1), (4, 256, 256), jnp.float32)
        _lenS = 256 - jax.random.randint(jax.random.fold_in(_rk, 7), (4,), 0, max(1, 256 // 4) + 1, jnp.int32)
        _lenS2 = 256 - jax.random.randint(jax.random.fold_in(_rk, 8), (4,), 0, max(1, 256 // 4) + 1, jnp.int32)
        _ctx_1024P = jax.random.normal(jax.random.fold_in(_rk, 11), (4, 16, 128), jnp.float32)
        _ctx_1024c = jax.random.dirichlet(jax.random.fold_in(_rk, 511), 0.3 * jnp.ones((16,), jnp.float32), (4, 256))
        _ctx_1024t = jnp.einsum('bsk,bkd->bsd', _ctx_1024c, _ctx_1024P)
        _ctx_1024t = _ctx_1024t * jax.lax.rsqrt(jnp.mean(jnp.square(_ctx_1024t)) + 1e-12) * 0.953939
        ctx_1024 = -0.000292821 + 1.00034 * (_ctx_1024t + 0.3 * jax.random.normal(jax.random.fold_in(_rk, 611), (4, 256, 128), jnp.float32))
        return (x, ctx_1024)
    x, ctx_1024 = _rec_inputs()

    def _L0_xattn_setup():
        import jax, jax.numpy as jnp
        import numpy as np
        import math
        B, L, DM = (2, 256, 128)
        DS, DC, EXP = (16, 4, 2)
        DI = EXP * DM
        DR = math.ceil(DM / 16)
        DT_MIN, DT_MAX, DT_FLOOR = (0.001, 0.1, 0.0001)

        def _ssm_forward(hidden_states, z, in_proj_w, conv_w, conv_b, x_proj_w, dt_proj_w, dt_proj_b, A_log, D):
            b = hidden_states.shape[0]
            x = jnp.einsum('ed,bld->bel', in_proj_w, hidden_states)
            xp = jnp.pad(x, ((0, 0), (0, 0), (DC - 1, 0)))
            xc = jax.lax.conv_general_dilated(xp, conv_w[:, None, :], window_strides=(1,), padding='VALID', dimension_numbers=('NCH', 'OIH', 'NCH'), feature_group_count=DI)
            u = jax.nn.silu(xc + conv_b[None, :, None])
            x_dbl = jnp.einsum('ke,bel->bkl', x_proj_w, u)
            dt_lo = x_dbl[:, :DR]
            Bm = x_dbl[:, DR:DR + DS]
            Cm = x_dbl[:, DR + DS:]
            delta = jax.nn.softplus(jnp.einsum('er,brl->bel', dt_proj_w, dt_lo) + dt_proj_b[None, :, None])
            A = -jnp.exp(A_log)

            def step(state, xs):
                d_t, B_t, C_t, u_t = xs
                dA = jnp.exp(d_t[..., None] * A)
                state = state * dA + (d_t * u_t)[..., None] * B_t[:, None, :]
                y_t = jnp.einsum('ben,bn->be', state, C_t)
                return (state, y_t)
            xs = (jnp.moveaxis(delta, -1, 0), jnp.moveaxis(Bm, -1, 0), jnp.moveaxis(Cm, -1, 0), jnp.moveaxis(u, -1, 0))
            state0 = jnp.zeros((b, DI, DS), delta.dtype)
            _, ys = jax.lax.scan(step, state0, xs)
            y = jnp.moveaxis(ys, 0, -1)
            y = y + D[None, :, None] * u
            y = y * jax.nn.silu(z)
            return jnp.swapaxes(y, 1, 2)
        key = jax.random.key(seed)
        ks = jax.random.split(key, 8)
        hidden_states = jax.random.normal(ks[0], (B, L, DM), jnp.float32)
        z = jax.random.normal(ks[1], (B, DI, L), jnp.float32)
        in_proj_w = jax.random.normal(ks[2], (DI, DM), jnp.float32) * DM ** (-0.5)
        conv_w = jax.random.normal(ks[3], (DI, DC), jnp.float32) * DC ** (-0.5)
        conv_b = jnp.zeros((DI,), jnp.float32)
        x_proj_w = jax.random.normal(ks[4], (DR + 2 * DS, DI), jnp.float32) * DI ** (-0.5)
        dt_std = DR ** (-0.5)
        dt_proj_w = jax.random.uniform(ks[5], (DI, DR), jnp.float32, -dt_std, dt_std)
        dt = jnp.exp(jax.random.uniform(ks[6], (DI,), jnp.float32) * (math.log(DT_MAX) - math.log(DT_MIN)) + math.log(DT_MIN))
        dt = jnp.clip(dt, DT_FLOOR)
        dt_proj_b = dt + jnp.log(-jnp.expm1(-dt))
        A_log = jnp.log(jnp.broadcast_to(jnp.arange(1, DS + 1, dtype=jnp.float32), (DI, DS)))
        D = jnp.ones((DI,), jnp.float32)
        return dict(hidden_states=hidden_states, z=z, in_proj_w=in_proj_w, conv_w=conv_w, conv_b=conv_b, x_proj_w=x_proj_w, dt_proj_w=dt_proj_w, dt_proj_b=dt_proj_b, A_log=A_log, D=D)
    _L0_xattn_all = _L0_xattn_setup()
    _L0_xattn_in = {k: v for k, v in _L0_xattn_all.items() if k in ('in_proj_w', 'conv_w', 'conv_b', 'x_proj_w', 'dt_proj_w', 'dt_proj_b', 'A_log', 'D')}
    del _L0_xattn_all

    def _L0_ffn_setup():
        import jax, jax.numpy as jnp
        import numpy as np
        E, TOPK, H, I = (8, 2, 256, 512)
        SOFTCAP = 30.0
        key = jax.random.key(seed)
        ks = jax.random.split(key, 5)
        s = 1.0 / np.sqrt(H)
        si = 1.0 / np.sqrt(I)
        return {'hidden_states': jax.random.normal(ks[0], (4, 256, H), jnp.float32), 'w_gate': jax.random.normal(ks[1], (H, E), jnp.float32) * s, 'w1': jax.random.normal(ks[2], (E, H, I), jnp.float32) * s, 'w3': jax.random.normal(ks[3], (E, H, I), jnp.float32) * s, 'w2': jax.random.normal(ks[4], (E, I, H), jnp.float32) * si}
    _L0_ffn_all = _L0_ffn_setup()
    _L0_ffn_in = {k: v for k, v in _L0_ffn_all.items() if k in ('w_gate', 'w1', 'w3', 'w2')}
    del _L0_ffn_all
    return {'x': x, 'ctx_1024': ctx_1024, 'L0_xattn_in_proj_w': _L0_xattn_in['in_proj_w'], 'L0_xattn_conv_w': _L0_xattn_in['conv_w'], 'L0_xattn_conv_b': _L0_xattn_in['conv_b'], 'L0_xattn_x_proj_w': _L0_xattn_in['x_proj_w'], 'L0_xattn_dt_proj_w': _L0_xattn_in['dt_proj_w'], 'L0_xattn_dt_proj_b': _L0_xattn_in['dt_proj_b'], 'L0_xattn_A_log': _L0_xattn_in['A_log'], 'L0_xattn_D': _L0_xattn_in['D'], 'L0_ffn_w_gate': _L0_ffn_in['w_gate'], 'L0_ffn_w1': _L0_ffn_in['w1'], 'L0_ffn_w3': _L0_ffn_in['w3'], 'L0_ffn_w2': _L0_ffn_in['w2']}

def reference(x, ctx_1024, L0_xattn_in_proj_w, L0_xattn_conv_w, L0_xattn_conv_b, L0_xattn_x_proj_w, L0_xattn_dt_proj_w, L0_xattn_dt_proj_b, L0_xattn_A_log, L0_xattn_D, L0_ffn_w_gate, L0_ffn_w1, L0_ffn_w3, L0_ffn_w2):
    import jax
    import jax.numpy as jnp

    def _L0_xattn_ref(hidden_states, z, in_proj_w, conv_w, conv_b, x_proj_w, dt_proj_w, dt_proj_b, A_log, D):
        import jax, jax.numpy as jnp
        import numpy as np
        import math
        B, L, DM = (2, 256, 128)
        DS, DC, EXP = (16, 4, 2)
        DI = EXP * DM
        DR = math.ceil(DM / 16)
        DT_MIN, DT_MAX, DT_FLOOR = (0.001, 0.1, 0.0001)

        def _ssm_forward(hidden_states, z, in_proj_w, conv_w, conv_b, x_proj_w, dt_proj_w, dt_proj_b, A_log, D):
            b = hidden_states.shape[0]
            x = jnp.einsum('ed,bld->bel', in_proj_w, hidden_states)
            xp = jnp.pad(x, ((0, 0), (0, 0), (DC - 1, 0)))
            xc = jax.lax.conv_general_dilated(xp, conv_w[:, None, :], window_strides=(1,), padding='VALID', dimension_numbers=('NCH', 'OIH', 'NCH'), feature_group_count=DI)
            u = jax.nn.silu(xc + conv_b[None, :, None])
            x_dbl = jnp.einsum('ke,bel->bkl', x_proj_w, u)
            dt_lo = x_dbl[:, :DR]
            Bm = x_dbl[:, DR:DR + DS]
            Cm = x_dbl[:, DR + DS:]
            delta = jax.nn.softplus(jnp.einsum('er,brl->bel', dt_proj_w, dt_lo) + dt_proj_b[None, :, None])
            A = -jnp.exp(A_log)

            def step(state, xs):
                d_t, B_t, C_t, u_t = xs
                dA = jnp.exp(d_t[..., None] * A)
                state = state * dA + (d_t * u_t)[..., None] * B_t[:, None, :]
                y_t = jnp.einsum('ben,bn->be', state, C_t)
                return (state, y_t)
            xs = (jnp.moveaxis(delta, -1, 0), jnp.moveaxis(Bm, -1, 0), jnp.moveaxis(Cm, -1, 0), jnp.moveaxis(u, -1, 0))
            state0 = jnp.zeros((b, DI, DS), delta.dtype)
            _, ys = jax.lax.scan(step, state0, xs)
            y = jnp.moveaxis(ys, 0, -1)
            y = y + D[None, :, None] * u
            y = y * jax.nn.silu(z)
            return jnp.swapaxes(y, 1, 2)
        return _ssm_forward(hidden_states, z, in_proj_w, conv_w, conv_b, x_proj_w, dt_proj_w, dt_proj_b, A_log, D)

    def _L0_ffn_ref(hidden_states, w_gate, w1, w3, w2):
        import jax, jax.numpy as jnp
        import numpy as np
        E, TOPK, H, I = (8, 2, 256, 512)
        SOFTCAP = 30.0
        orig_shape = hidden_states.shape
        x = hidden_states.reshape(-1, H)
        logits = x @ w_gate
        logits = SOFTCAP * jnp.tanh(logits / SOFTCAP)
        probs = jax.nn.softmax(logits, axis=-1)
        _, idx = jax.lax.top_k(probs, TOPK)
        mask = jax.nn.one_hot(idx, E, dtype=probs.dtype).sum(-2)
        weights = probs * mask
        out = jnp.zeros_like(x)
        for e in range(E):
            h = jax.nn.silu(x @ w1[e]) * (x @ w3[e])
            out = out + h @ w2[e] * weights[:, e:e + 1]
        return out.reshape(orig_shape)
    x = x + _L0_xattn_ref(ctx_1024, _layernorm(x, axis=-1), L0_xattn_in_proj_w, L0_xattn_conv_w, L0_xattn_conv_b, L0_xattn_x_proj_w, L0_xattn_dt_proj_w, L0_xattn_dt_proj_b, L0_xattn_A_log, L0_xattn_D)
    x = x + _L0_ffn_ref(_layernorm(x, axis=-1), L0_ffn_w_gate, L0_ffn_w1, L0_ffn_w3, L0_ffn_w2)
    return x

_drawn_inputs = setup_inputs


def setup_inputs(seed=0):
    import zlib

    import numpy as np

    out = dict(_drawn_inputs(seed))
    spreads = {'L0_xattn_conv_b': (0.0, 0.1), 'L0_xattn_D': (1.0, 0.2)}
    factors = {'L0_xattn_dt_proj_w': 4.204}
    for name, (base, spread) in spreads.items():
        noise = np.random.default_rng([zlib.crc32(name.encode()), seed]).standard_normal(out[name].shape)
        drawn = base * np.exp(spread * noise) if base else spread * noise
        out[name] = jnp.asarray(drawn.astype(out[name].dtype))
    for name, factor in factors.items():
        out[name] = (out[name] * factor).astype(out[name].dtype)
    return out
```

```python
from contextlib import ExitStack

import concourse.bass as bass
from concourse import mybir

P = 128
ALU = mybir.AluOpType
ACT = mybir.ActivationFunctionType
F32 = mybir.dt.float32
F32R = mybir.dt.float32r
BF16 = mybir.dt.bfloat16
AX_X = mybir.AxisListType.X

EPS = 1e-5
SOFTCAP = 30.0
TOPK = 2
RS = 6


def xattn_ffn(nc, x, ctx_t, in_proj_t, conv_w_t, channel_rows, x_proj_rows, dt_proj_t, w_gate, w1, w3, w2, out):
    DM, B, L = ctx_t.shape
    DI = in_proj_t.shape[1]
    TAPS = conv_w_t.shape[0]
    DR = dt_proj_t.shape[0]
    DS = channel_rows.shape[1] - 3
    E, H, I = w1.shape
    assert DM == P and DI == L == H == 2 * P and DS == 16
    PAD = TAPS - 1
    ET = DI // P
    PAIRS = B // 2
    T = 2 * L
    NT = B * L // P
    N2 = DS // 2
    BCR = 2 * DS
    DT0 = 3 * BCR
    HK = H // P
    IT = I // P
    TG = B * L // T
    TT = T // P
    UE = TG * IT
    UB = 2 * UE
    WCOLS = 2 * HK * I + IT * H
    W3_AT, W2_AT = HK * I, 2 * HK * I

    with ExitStack() as ctx:
        def sb(name, shape, dt=F32):
            return ctx.enter_context(nc.sbuf_tensor(name, shape, dt))

        def sem(name):
            return ctx.enter_context(nc.semaphore(name))

        ctx_pad = sb("ctx_pad", [P, B, L + PAD])
        inw = sb("inw", [P, DI])
        tapw = sb("tapw", [P, TAPS, DI])
        channel = sb("channel", [P, ET, 3 + DS])
        conv_bias, dt_bias, dskip, alog = channel[:, :, 0], channel[:, :, 1], channel[:, :, 2], channel[:, :, 3:]
        half_conv_bias = sb("half_conv_bias", [P, ET])
        xpw = sb("xpw", [P, ET, DT0 + DR])
        dtw = sb("dtw", [P, DI])
        exp_alog = sb("exp_alog", [P, ET, DS])
        neg_a = sb("neg_a", [P, ET, DS])
        diag_d = sb("diag_d", [P, ET, P])
        ident = sb("ident", [P, P])
        ident_bc = sb("ident_bc", [P, BCR], BF16)
        select = sb("select", [P, BCR, P], BF16)
        xs = sb("xs", [P, NT, H])
        wg = sb("wg", [P, HK, E])
        wg_hi = sb("wg_hi", [P, HK, E], F32R)
        wg_lo = sb("wg_lo", [P, HK, E], F32R)

        tanh_t = sb("tanh_t", [P, PAIRS * ET, T])
        u = sb("u", [P, PAIRS * ET, T])
        convw = u[:, 0:2].rearrange("p n (k e) -> p (n k) e", e=DI)
        bc_round = sb("bc_round", [P, T], BF16)
        bc_mid = sb("bc_mid", [P, T], BF16)
        bc = sb("bc", [P, PAIRS, T], BF16)
        dt_lo = sb("dt_lo", [P, PAIRS, T])
        delta = sb("delta", [P, PAIRS * ET, 2, L])
        du = sb("du", [P, PAIRS * ET, T])

        stats = sb("stats", [P, NT, 6])
        mv = sb("mv", [P, NT, 2])
        rstd = sb("rstd", [P, NT])
        inv_var = sb("inv_var", [P, NT])
        half_rstd = sb("half_rstd", [P, NT])
        neg_half_mr = sb("neg_half_mr", [P, NT])
        zt = sb("zt", [P, NT, L])

        decay = sb("decay", [P, ET, 2, 2, L])
        drive = sb("drive", [P, ET, 2, T])
        state = sb("state", [P, ET, 2, T])
        c_rows = sb("c_rows", [P, 2, 2, T])
        prod = sb("prod", [P, ET, 2, T])
        sp_exp, sp_abs, sp_ln = state[:, 0], state[:, 1], drive[:, 0]
        sp_max, sp_round = drive[:, 1, 0], drive[:, 1, 1]
        half_t, bc_rest = c_rows[:, 0, 0], c_rows[:, 0, 1]
        z = prod[:].rearrange("p a b (c l) -> p (a b c) l", l=L)
        yg = tanh_t[:].rearrange("p n (b l) -> p n b l", b=2)

        stats2 = sb("stats2", [P, NT, 6])
        mv2 = sb("mv2", [P, NT, 2])
        rstd2 = sb("rstd2", [P, NT])
        inv_var2 = sb("inv_var2", [P, NT])
        xn = c_rows[:].rearrange("p a b (c h) -> p (a b c) h", h=H)
        xt_hi = sb("xt_hi", [P, HK, B * L], F32R)
        xt_lo = sb("xt_lo", [P, HK, B * L], F32R)
        lg_tanh = sb("lg_tanh", [P, NT, E])
        lg_max = sb("lg_max", [P, NT])
        lg_exp = sb("lg_exp", [P, NT, E])
        lg_sum = sb("lg_sum", [P, NT])
        probs = sb("probs", [P, NT, E + 8 - TOPK])
        top8 = sb("top8", [P, NT, 8])
        chosen = sb("chosen", [P, NT, 8])
        others = sb("others", [P, NT, E + 8 - TOPK])
        weight = sb("weight", [P, NT, E])

        w_raw = sb("w_raw", [P, WCOLS])
        w_hi = sb("w_hi", [P, 2, WCOLS], F32R)
        w_lo = sb("w_lo", [P, 2, WCOLS], F32R)
        g_tanh, g_silu2 = state[:, 0], state[:, 1]
        hid = drive[:, 0]
        hid_hi = sb("hid_hi", [P, 2, T], F32R)
        hid_lo = sb("hid_lo", [P, 2, T], F32R)

        ps = ctx.enter_context(nc.psum_tensor("ps", [P, 8, T], F32))

        s_small = sem("small_landed")
        s_vec = sem("vectors_landed")
        s_ctx = sem("ctx_landed")
        s_x = sem("x_landed")
        s_raw = sem("raw_landed")
        s_inw = sem("in_proj_landed")
        s_out = sem("out_stored")
        s_const = sem("constants_built")
        s_pad = sem("pads_cleared")
        s_tap = sem("tap_weights_ready")
        s_const_v = sem("vector_constants_ready")
        s_alog = sem("exp_alog_ready")
        s_conv = sem("conv_done")
        s_tanh = sem("conv_tanh_done")
        s_half = sem("conv_half_done")
        s_selm = sem("select_ready")
        s_u = sem("u_done")
        s_xp = sem("x_proj_done")
        s_bca = sem("bc_parts_scalar")
        s_bcv = sem("bc_parts_vector")
        s_dtlo = sem("dt_lo_ready")
        s_dt = sem("dt_proj_done")
        s_spa = sem("softplus_scalar_steps")
        s_spv = sem("softplus_vector_steps")
        s_du = sem("du_ready")
        s_ln1 = sem("ln1_steps")
        s_root = sem("variance_root_done")
        s_zt = sem("z_tanh_done")
        s_gz = sem("gated_z_ready")
        s_rows = sem("bc_rows_broadcast")
        s_crow = sem("c_rows_copied")
        s_decay = sem("decay_ready")
        s_drive = sem("drive_ready")
        s_state = sem("state_ready")
        s_prod = sem("prod_ready")
        s_sum = sem("prod_summed")
        s_open = sem("y_opened")
        s_yg = sem("yg_ready")
        s_yt = sem("y_turned")
        s_x1 = sem("x1_ready")
        s_ln2 = sem("ln2_steps")
        s_xn = sem("xn_ready")
        s_xt = sem("xn_turned")
        s_xhi = sem("xt_hi_ready")
        s_xlo = sem("xt_lo_ready")
        s_lg = sem("logits_done")
        s_rta = sem("router_scalar_steps")
        s_rtv = sem("router_vector_steps")
        s_whi = sem("w_hi_ready")
        s_wlo = sem("w_lo_ready")
        s_wg = sem("gate_weights_split")
        s_gate = sem("gate_done")
        s_up = sem("up_done")
        s_gt = sem("gate_tanh_done")
        s_gs = sem("gate_silu_done")
        s_hid = sem("hid_done")
        s_hhi = sem("hid_hi_done")
        s_hlo = sem("hid_lo_done")
        s_down = sem("down_unit_done")
        s_acc = sem("down_added")

        x_rows = x.rearrange("b (t p) h -> p (b t) h", p=P)
        out_rows = out.rearrange("b (t p) h -> p (b t) h", p=P)
        w1_d = w1.rearrange("e (k p) i -> e p k i", p=P)
        w3_d = w3.rearrange("e (k p) i -> e p k i", p=P)
        w2_d = w2.rearrange("e (k p) h -> e p k h", p=P)

        block = ctx.enter_context(nc.Block())

        @block.sync
        def _(sp):
            sp.dma_start(inw[:], in_proj_t).then_inc(s_inw, 16)
            sp.dma_start(convw, conv_w_t.rearrange("(o k) e -> o k e", o=1).to_broadcast((P, TAPS, DI))).then_inc(s_inw, 16)
            for b in range(B):
                sp.dma_start(ctx_pad[:, b, PAD:], ctx_t[:, b]).then_inc(s_ctx, 16)
            sp.dma_start(xpw[:], x_proj_rows.rearrange("(k p) c -> p k c", p=P)).then_inc(s_small, 16)
            sp.dma_start(dtw[DT0:DT0 + DR, :], dt_proj_t).then_inc(s_small, 16)
            sp.dma_start(wg[:], w_gate.rearrange("(k p) e -> p k e", p=P)).then_inc(s_small, 16)

            def load_expert(e):
                for at, w, k in ((0, w1_d, HK), (W3_AT, w3_d, HK), (W2_AT, w2_d, IT)):
                    sp.dma_start(w_raw[:, at:at + WCOLS // 3].rearrange("p (k i) -> p k i", k=k),
                                 w[e].rearrange("o p k i -> (o p) k i")).then_inc(s_raw, 16)

            load_expert(slice(0, 1))
            with sp.Fori(0, E - 1) as e:
                sp.wait_ge(s_whi, IT * e + IT)
                sp.wait_ge(s_wlo, IT * e + IT)
                load_expert(bass.ds(e + 1, 1))
            for g in range(TG):
                sp.wait_ge(s_acc, (E - 1) * TG * TT + (g + 1) * TT)
                sp.dma_start(out_rows[:, g * TT:(g + 1) * TT], xs[:, g * TT:(g + 1) * TT]).then_inc(s_out, 16)
            sp.wait_ge(s_out, 16 * TG)

        def over_state_pairs(engine, p, body):
            body(0)
            with engine.Fori(1, N2 // 2 - 1) as i:
                body(i)
            body(N2 // 2 - 1)

        def over_expert_pairs(engine, body):
            body(0, True, False)
            with engine.Fori(1, E // 2 - 1) as i:
                body(i, False, False)
            body(E // 2 - 1, False, True)

        @block.gpsimd
        def _(pool):
            pool.memset(ctx_pad[:, :, 0:PAD], 0.0).then_inc(s_pad, 1)
            pool.memset(ident_bc[:], 0.0).then_inc(s_pad, 1)
            pool.memset(ident[:], 0.0).then_inc(s_pad, 1)
            pool.wait_ge(s_pad, 2)
            for copy in range(3):
                pool.affine_select(out=ident_bc[:], in_=ident_bc[:], compare_op=ALU.not_equal, fill=1.0,
                                   base=-copy * BCR, pattern=[[-1, BCR]], channel_multiplier=1).then_inc(s_const, 1)
                pool.wait_ge(s_const, copy + 1)
            pool.wait_ge(s_pad, 3)
            pool.affine_select(out=ident[:], in_=ident[:], compare_op=ALU.not_equal, fill=1.0, base=0,
                               pattern=[[-1, P]], channel_multiplier=1).then_inc(s_const, 1)
            pool.memset(decay[:, :, :, :, 0:1].rearrange("p a b c o -> p (a b c) o"), 0.0).then_inc(s_pad, 1)
            pool.memset(probs[:], -1.0).then_inc(s_pad, 1)
            pool.memset(chosen[:], -1.0).then_inc(s_pad, 1)

            pool.wait_ge(s_gz, 1)
            for p in range(PAIRS):
                def c_products(i):
                    for par in range(2):
                        n2 = 2 * i + (p * N2 + par)
                        for et in range(ET):
                            n = ET * n2 + et
                            pool.wait_ge(s_state, n + 1)
                            pool.wait_ge(s_crow, n2 + 1)
                            if not (p == 0 and isinstance(i, int) and i == 0 and par == 0):
                                pool.wait_ge(s_sum, n - (ET - 1))
                            pool.tensor_tensor(prod[:, et], state[:, et], c_rows[:, par], ALU.mult).then_inc(s_prod, 1)
                over_state_pairs(pool, p, c_products)

            def split_low(e, j, q):
                n = WCOLS // IT
                pool.wait_ge(s_whi, IT * e + (q + 1))
                pool.tensor_tensor(w_lo[:, j, q * n:(q + 1) * n], w_raw[:, q * n:(q + 1) * n],
                                   w_hi[:, j, q * n:(q + 1) * n].bitcast(F32), ALU.subtract).then_inc(s_wlo, 1)

            for q in range(IT):
                split_low(0, 0, q)

            def expert_pair(i, first, last):
                for v in range(UB):
                    n = UB * i + v
                    pool.wait_ge(s_hhi, n + 1)
                    if not first or v >= 2:
                        pool.wait_ge(s_down, n - 1)
                    pool.tensor_tensor(hid_lo[:, v % 2], hid[:, v % 2], hid_hi[:, v % 2].bitcast(F32),
                                       ALU.subtract).then_inc(s_hlo, 1)
                    if 2 <= v % UE < 2 + IT and (v < UE or not last):
                        split_low(2 * i + (1 + v // UE), 1 - v // UE, v % UE - 2)

            over_expert_pairs(pool, expert_pair)

        @block.scalar
        def _(act):
            act.dma_start(channel[:], channel_rows.rearrange("(k p) c -> p k c", p=P)).then_inc(s_vec, 16)
            for g in range(TG):
                act.dma_start(xs[:, g * TT:(g + 1) * TT], x_rows[:, g * TT:(g + 1) * TT]).then_inc(s_x, 16)
            act.wait_ge(s_vec, 16)
            act.activation(exp_alog[:], alog, ACT.Exp).then_inc(s_alog, 1)

            act.wait_ge(s_ln1, 2 * NT + 2)
            act.activation(rstd[:], inv_var[:], ACT.Sqrt).then_inc(s_root, 1)
            act.wait_ge(s_const_v, 1)
            for n in range(PAIRS * ET):
                act.wait_ge(s_conv, n + 1)
                act.activation(tanh_t[:, n], ps[:, 2 + n], ACT.Tanh, scale=0.5,
                               bias=half_conv_bias[:, n % ET:n % ET + 1]).then_inc(s_tanh, 1)
            act.wait_ge(s_ln1, 2 * NT + RS + 2)
            for t in range(NT):
                act.activation(zt[:, t], xs[:, t], ACT.Tanh, scale=half_rstd[:, t:t + 1],
                               bias=neg_half_mr[:, t:t + 1]).then_inc(s_zt, 1)
            for p in range(PAIRS):
                act.wait_ge(s_xp, p + 1)
                if p:
                    act.wait_ge(s_bcv, 3 * p)
                act.activation(bc_round[0:DT0], ps[0:DT0, 6 + p], ACT.Copy).then_inc(s_bca, 1)
                act.activation(bc[0:BCR, p], ps[0:BCR, 6 + p], ACT.Copy).then_inc(s_bca, 1)
                act.activation(dt_lo[DT0:DT0 + DR, p], ps[DT0:DT0 + DR, 6 + p], ACT.Copy).then_inc(s_dtlo, 1)
                act.wait_ge(s_bcv, 3 * p + 1)
                act.activation(bc[BCR:2 * BCR, p], bc_rest[BCR:2 * BCR], ACT.Copy).then_inc(s_bca, 1)
                for et in range(ET):
                    act.wait_ge(s_dt, p * ET + et + 1)
                    act.activation(sp_abs[:, et], ps[:, 2 * p + et], ACT.Abs, bias=dt_bias[:, et:et + 1]).then_inc(s_spa, 1)
                for et in range(ET):
                    act.wait_ge(s_spa, 6 * p + et + 1)
                    if p:
                        act.wait_ge(s_spv, 4 * (et + 1))
                    act.activation(sp_exp[:, et], sp_abs[:, et], ACT.Exp, scale=-1.0).then_inc(s_spa, 1)
                for et in range(ET):
                    act.wait_ge(s_spa, 6 * p + ET + et + 1)
                    if p:
                        act.wait_ge(s_du, et + 1)
                    act.activation(sp_ln[:, et], sp_exp[:, et], ACT.Ln, bias=1.0).then_inc(s_spa, 1)

            neg_a_q = neg_a[:].rearrange("p k (i q) -> p k i q", q=4)
            act.wait_ge(s_pad, 4)
            act.wait_ge(s_const_v, 4)
            act.wait_ge(s_du, PAIRS * ET)
            for p in range(PAIRS):
                def decays(i):
                    for par in range(2):
                        n2 = 2 * i + (p * N2 + par)
                        start = p == 0 and isinstance(i, int) and i == 0
                        act.wait_ge(s_rows, n2 + 1)
                        if not start:
                            act.wait_ge(s_prod, ET * n2 - ET)
                        act.activation(c_rows[:, par], ps[:, 6:8], ACT.Copy).then_inc(s_crow, 1)
                        for et in range(ET):
                            if not (start and par == 0):
                                act.wait_ge(s_state, ET * n2 + et - (ET - 1))
                            for j in range(2):
                                act.activation(decay[:, et, j, :, 1:], delta[:, p * ET + et, :, 1:], ACT.Exp,
                                               scale=neg_a_q[:, et, i, 2 * par + j:2 * par + j + 1]).then_inc(s_decay, 1)
                over_state_pairs(act, p, decays)

            def split_high(j, q):
                n = WCOLS // IT
                act.activation(w_hi[:, j, q * n:(q + 1) * n], w_raw[:, q * n:(q + 1) * n], ACT.Copy).then_inc(s_whi, 1)

            act.wait_ge(s_raw, 48)
            for q in range(IT):
                split_high(0, q)
            act.wait_ge(s_ln2, 2 * NT + 2)
            act.activation(rstd2[:], inv_var2[:], ACT.Sqrt).then_inc(s_root, 1)
            for n in range(HK * TG):
                act.wait_ge(s_xt, n + 1)
                act.activation(xt_hi[:, n // TG, n % TG * T:(n % TG + 1) * T], ps[:, n], ACT.Copy).then_inc(s_xhi, 1)
            act.wait_ge(s_lg, 1)
            act.activation(lg_tanh[:], ps[:, 4, 0:NT * E].rearrange("p (t e) -> p t e", e=E), ACT.Tanh,
                           scale=1.0 / SOFTCAP).then_inc(s_rta, 1)
            act.wait_ge(s_rtv, 2)
            act.activation(lg_exp[:], lg_exp[:], ACT.Exp, scale=SOFTCAP).then_inc(s_rta, 1)

            def expert_pair(i, first, last):
                for v in range(UB):
                    n = UB * i + v
                    act.wait_ge(s_gate, n + 1)
                    if not first or v >= 2:
                        act.wait_ge(s_gs, n - 1)
                    act.activation(g_tanh[:, v % 2], ps[:, v % 2 * 2], ACT.Tanh, scale=0.5).then_inc(s_gt, 1)
                    if 2 <= v % UE < 2 + IT and (v < UE or not last):
                        if v % UE == 2:
                            act.wait_ge(s_raw, 96 * i + (96 + 48 * (v // UE)))
                            if not first or v >= UE:
                                act.wait_ge(s_down, UB * i + v // UE * UE)
                        split_high(1 - v // UE, v % UE - 2)
                    act.wait_ge(s_hid, n + 1)
                    if not first or v >= 2:
                        act.wait_ge(s_down, n - 1)
                    act.activation(hid_hi[:, v % 2], hid[:, v % 2], ACT.Copy).then_inc(s_hhi, 1)

            over_expert_pairs(act, expert_pair)

        @block.tensor
        def _(pe):
            pe.wait_ge(s_tap, 1)
            pe.wait_ge(s_pad, 1)
            pe.wait_ge(s_ctx, 16 * B)
            for n in range(PAIRS * ET):
                p, et = n // ET, n % ET
                for k in range(TAPS):
                    mm = pe.matmul(ps[:, 2 + n].rearrange("p (b l) -> p b l", b=2), tapw[:, k, et * P:(et + 1) * P],
                                   ctx_pad[:, 2 * p:2 * p + 2, k:k + L], start=(k == 0), stop=(k == TAPS - 1))
                mm.then_inc(s_conv, 1)
            pe.wait_ge(s_small, 48)
            for p in range(PAIRS):
                for k in range(ET):
                    pe.wait_ge(s_u, p * ET + k + 1)
                    mm = pe.matmul(ps[0:DT0 + DR, 6 + p], xpw[:, k, :], u[:, p * ET + k], start=(k == 0), stop=(k == ET - 1))
                mm.then_inc(s_xp, 1)
            for p in range(PAIRS):
                pe.wait_ge(s_dtlo, p + 1)
                for et in range(ET):
                    pe.matmul(ps[:, 2 * p + et], dtw[DT0:DT0 + DR, et * P:(et + 1) * P], dt_lo[DT0:DT0 + DR, p],
                              start=True, stop=True).then_inc(s_dt, 1)

            def broadcast_rows(p, i, par):
                for at, bank in ((0, 2 + 2 * par), (DS, 6)):
                    for j in range(2):
                        row = 4 * i + (at + 2 * par + j)
                        sel = select[0:DT0, row, :] if isinstance(row, int) else \
                            select[0:DT0, bass.ds(row, 1), :].rearrange("p o m -> p (o m)")
                        mm = pe.matmul(ps[:, bank + j], sel, bc[0:DT0, p], start=True, stop=True)
                mm.then_inc(s_rows, 1)

            pe.wait_ge(s_selm, 1)
            pe.wait_ge(s_bca, 3 * PAIRS)
            pe.wait_ge(s_bcv, 3 * PAIRS)
            pe.wait_ge(s_du, PAIRS * ET)
            broadcast_rows(0, 0, 0)
            pe.wait_ge(s_const_v, 3)
            for p in range(PAIRS):
                for et in range(ET):
                    if p:
                        pe.wait_ge(s_yg, ET * p)
                    pe.matmul(ps[:, et], diag_d[:, et], u[:, p * ET + et], start=True, stop=False,
                              skip_group_check=True)

                def sums(i):
                    for par in range(2):
                        n2 = 2 * i + (p * N2 + par)
                        final = par == 1 and isinstance(i, int) and i == N2 // 2 - 1
                        if not (final and p == PAIRS - 1):
                            if not (p == 0 and isinstance(i, int) and i == 0 and par == 0):
                                pe.wait_ge(s_drive, ET * n2)
                            pe.wait_ge(s_crow, n2 + 1)
                            if final:
                                broadcast_rows(p + 1, 0, 0)
                            elif par == 0:
                                broadcast_rows(p, i, 1)
                            else:
                                broadcast_rows(p, i + 1, 0)
                        for et in range(ET):
                            pe.wait_ge(s_prod, ET * n2 + (et + 1))
                            for j in range(2):
                                mm = pe.matmul(ps[:, et], ident[:], prod[:, et, j], start=False, stop=final and j == 1,
                                               skip_group_check=True)
                            mm.then_inc(s_sum, 1)
                over_state_pairs(pe, p, sums)

            for t in range(NT):
                p, b, half = t // 4, t // 2 % 2, t % 2
                pe.wait_ge(s_yg, ET * (p + 1))
                for et in range(ET):
                    mm = pe.transpose(ps[:, 2 + t // 2, half * DI + et * P:half * DI + (et + 1) * P],
                                      yg[:, p * ET + et, b, half * P:(half + 1) * P], ident[:])
                if half:
                    mm.then_inc(s_yt, 1)
            for n in range(HK * TG):
                k, g = n // TG, n % TG
                pe.wait_ge(s_xn, NT)
                for t in range(TT):
                    mm = pe.transpose(ps[:, n, t * P:(t + 1) * P], xn[:, g * TT + t, k * P:(k + 1) * P], ident[:])
                mm.then_inc(s_xt, 1)
            pe.wait_ge(s_wg, 2)
            pe.wait_ge(s_xhi, HK * TG)
            pe.wait_ge(s_xlo, HK * TG)
            for t in range(NT):
                for k in range(HK):
                    for m, (xa, wa) in enumerate(((xt_hi, wg_hi), (xt_hi, wg_lo), (xt_lo, wg_hi), (xt_lo, wg_lo))):
                        mm = pe.matmul(ps[:, 4, t * E:(t + 1) * E], xa[:, k, t * P:(t + 1) * P], wa[:, k],
                                       start=(k == 0 and m == 0), stop=(k == HK - 1 and m == 3))
            mm.then_inc(s_lg, 1)

            w1_of = lambda w, j, k, it: w[:, j, k * I + it * P:k * I + (it + 1) * P]
            w3_of = lambda w, j, k, it: w[:, j, W3_AT + k * I + it * P:W3_AT + k * I + (it + 1) * P]
            w2_of = lambda w, j, it: w[:, j, W2_AT + it * H:W2_AT + (it + 1) * H]

            def gate_up(i, v, first):
                n = UB * i + v
                j, g, it, par = v // UE % 2, v // IT % TG, v % IT, v % 2
                if v % UE == 0:
                    pe.wait_ge(s_wlo, 2 * IT * i + (v // UE * IT + IT - 1))
                for made, of, bank, freed in ((s_gate, w1_of, 2 * par, s_gs), (s_up, w3_of, 2 * par + 1, s_hid)):
                    if not (first and v < 2):
                        pe.wait_ge(freed, n - 1)
                    for k in range(HK):
                        for m, (wa, xa) in enumerate(((w_hi, xt_hi), (w_hi, xt_lo), (w_lo, xt_hi))):
                            mm = pe.matmul(ps[:, bank], of(wa, j, k, it), xa[:, k, g * T:(g + 1) * T],
                                           start=(k == 0 and m == 0), stop=(k == HK - 1 and m == 2))
                    mm.then_inc(made, 1)

            def down(i, v, first):
                n = UB * i + v
                j, g, it, par = v // UE, v // IT % TG, v % IT, v % 2
                if v % UE == 0:
                    pe.wait_ge(s_wlo, 2 * IT * i + (j * IT + IT))
                if it == 0 and not (first and j == 0):
                    pe.wait_ge(s_acc, 2 * TG * TT * i + ((j - 1) * TG * TT + (g + 1) * TT))
                pe.wait_ge(s_hhi, n + 1)
                pe.wait_ge(s_hlo, n + 1)
                for t in range(TT):
                    for m, (ha, wa) in enumerate(((hid_hi, w_hi), (hid_hi, w_lo), (hid_lo, w_hi))):
                        mm = pe.matmul(ps[:, 4 + 2 * g + t // 2, t % 2 * H:(t % 2 + 1) * H], ha[:, par, t * P:(t + 1) * P],
                                       w2_of(wa, j, it), start=(it == 0 and m == 0 and t % 2 == 0),
                                       stop=(it == IT - 1 and m == 2), skip_group_check=True)
                mm.then_inc(s_down, 1)

            pe.wait_ge(s_rta, 1)
            gate_up(0, 0, True)
            gate_up(0, 1, True)

            def expert_pair(i, first, last):
                for v in range(UB):
                    if v + 2 < UB or not last:
                        gate_up(i, v + 2, first)
                    down(i, v, first)

            over_expert_pairs(pe, expert_pair)

        @block.vector
        def _(dve):
            dve.wait_ge(s_vec, 16)
            dve.tensor_scalar(half_conv_bias[:], conv_bias, 0.5, None, ALU.mult).then_inc(s_const_v, 1)
            dve.wait_ge(s_inw, 32)
            dve.tensor_tensor(tapw[:], convw, inw[:].unsqueeze(1).to_broadcast((P, TAPS, DI)), ALU.mult).then_inc(s_tap, 1)
            dve.wait_ge(s_const, 4)
            for et in range(ET):
                dve.tensor_scalar(diag_d[:, et], ident[:], dskip[:, et:et + 1], None, ALU.mult).then_inc(s_const_v, 1)
            dve.tensor_copy(select[:], ident_bc[:].unsqueeze(2).to_broadcast((P, BCR, P))).then_inc(s_selm, 1)
            dve.wait_ge(s_alog, 1)
            dve.tensor_scalar(neg_a[:], exp_alog[:], -1.0, None, ALU.mult).then_inc(s_const_v, 1)

            def inverse_root(r, m, inv, steps, turn):
                at = 2 * NT
                dve.wait_ge(steps, at)
                dve.tensor_scalar(m[:, :, 1], m[:, :, 1], EPS, None, ALU.add).then_inc(steps, 1)
                dve.wait_ge(steps, at + 1)
                dve.reciprocal(inv[:], m[:, :, 1]).then_inc(steps, 1)
                dve.wait_ge(s_root, turn)
                dve.tensor_tensor(inv[:], r[:], r[:], ALU.mult).then_inc(steps, 1)
                dve.wait_ge(steps, at + 3)
                dve.tensor_tensor(inv[:], inv[:], m[:, :, 1], ALU.mult).then_inc(steps, 1)
                dve.wait_ge(steps, at + 4)
                dve.tensor_scalar(inv[:], inv[:], -0.5, 1.5, ALU.mult, ALU.add).then_inc(steps, 1)
                dve.wait_ge(steps, at + 5)
                dve.tensor_tensor(r[:], r[:], inv[:], ALU.mult).then_inc(steps, 1)
                dve.wait_ge(steps, at + RS)

            dve.wait_ge(s_x, 16 * TG)
            for t in range(NT):
                dve.bn_stats(stats[:, t], xs[:, t]).then_inc(s_ln1, 1)
            for t in range(NT):
                dve.wait_ge(s_ln1, t + 1)
                dve.bn_aggr(mv[:, t], stats[:, t]).then_inc(s_ln1, 1)
            inverse_root(rstd, mv, inv_var, s_ln1, 1)
            dve.tensor_scalar(half_rstd[:], rstd[:], 0.5, None, ALU.mult).then_inc(s_ln1, 1)
            dve.wait_ge(s_ln1, 2 * NT + RS + 1)
            dve.scalar_tensor_tensor(neg_half_mr[:], mv[:, :, 0], -1.0, half_rstd[:], ALU.mult, ALU.mult).then_inc(s_ln1, 1)
            for t in range(NT):
                dve.tensor_scalar(z[:, t], xs[:, t], mv[:, t, 0:1], rstd[:, t:t + 1], ALU.subtract, ALU.mult).then_inc(s_ln1, 1)

            for n in range(PAIRS * ET):
                if n:
                    dve.wait_ge(s_u, n)
                dve.wait_ge(s_tanh, n + 1)
                dve.tensor_scalar(half_t, ps[:, 2 + n], conv_bias[:, n % ET:n % ET + 1], 0.5, ALU.add, ALU.mult).then_inc(s_half, 1)
                dve.wait_ge(s_half, n + 1)
                dve.scalar_tensor_tensor(u[:, n], tanh_t[:, n], 1.0, half_t, ALU.add, ALU.mult).then_inc(s_u, 1)

            for p in range(PAIRS):
                dve.wait_ge(s_bca, 3 * p + 2)
                dve.wait_ge(s_dtlo, p + 1)
                dve.wait_ge(s_u, PAIRS * ET)
                if p:
                    dve.wait_ge(s_bca, 3 * p)
                    dve.wait_ge(s_bcv, 3 * p)
                dve.tensor_tensor(bc_rest[0:DT0], ps[0:DT0, 6 + p], bc_round[0:DT0], ALU.subtract).then_inc(s_bcv, 1)
                dve.wait_ge(s_bcv, 3 * p + 1)
                dve.tensor_copy(bc_mid[2 * BCR:DT0], bc_rest[2 * BCR:DT0]).then_inc(s_bcv, 1)
                dve.wait_ge(s_bcv, 3 * p + 2)
                dve.tensor_tensor(bc[2 * BCR:DT0, p], bc_rest[2 * BCR:DT0], bc_mid[2 * BCR:DT0], ALU.subtract).then_inc(s_bcv, 1)
                for et in range(ET):
                    n = p * ET + et
                    dve.wait_ge(s_spa, 6 * p + et + 1)
                    if n:
                        dve.wait_ge(s_spv, 5 * n)
                        dve.wait_ge(s_du, n)
                    dve.tensor_scalar(sp_max, ps[:, 2 * p + et], dt_bias[:, et:et + 1], 0.0, ALU.add, ALU.max).then_inc(s_spv, 1)
                    dve.wait_ge(s_spa, 6 * p + ET + et + 1)
                    dve.tensor_scalar(sp_round, sp_exp[:, et], 1.0, -1.0, ALU.add, ALU.add).then_inc(s_spv, 1)
                    dve.wait_ge(s_spv, 5 * n + 2)
                    dve.tensor_tensor(sp_round, sp_exp[:, et], sp_round, ALU.subtract).then_inc(s_spv, 1)
                    dve.wait_ge(s_spv, 5 * n + 3)
                    dve.tensor_tensor(sp_max, sp_max, sp_round, ALU.add).then_inc(s_spv, 1)
                    dve.wait_ge(s_spv, 5 * n + 4)
                    dve.wait_ge(s_spa, 6 * p + 2 * ET + et + 1)
                    flat = delta[:, n].rearrange("p b l -> p (b l)")
                    dve.tensor_tensor(flat, sp_max, sp_ln[:, et], ALU.add).then_inc(s_spv, 1)
                    dve.wait_ge(s_spv, 5 * n + 5)
                    dve.tensor_tensor(du[:, n], flat, u[:, n], ALU.mult).then_inc(s_du, 1)
            dve.wait_ge(s_zt, NT)
            dve.wait_ge(s_ln1, 3 * NT + RS + 2)
            dve.scalar_tensor_tensor(zt[:], zt[:], 1.0, z, ALU.add, ALU.mult).then_inc(s_gz, 1)

            gz = zt[:].rearrange("p (q b k) l -> p q b k l", q=PAIRS, b=2)

            def gate_y(p):
                for et in range(ET):
                    dve.wait_ge(s_sum, (p + 1) * N2 * ET)
                    dve.scalar_tensor_tensor(yg[:, p * ET + et], ps[:, et].rearrange("p (b l) -> p b l", b=2), 0.5,
                                             gz[:, p, :, et], ALU.mult, ALU.mult).then_inc(s_yg, 1)

            dve.wait_ge(s_du, PAIRS * ET)
            dve.wait_ge(s_gz, 1)
            for p in range(PAIRS):
                def scans(i):
                    for par in range(2):
                        n2 = 2 * i + (p * N2 + par)
                        start = p == 0 and isinstance(i, int) and i == 0 and par == 0
                        dve.wait_ge(s_rows, n2 + 1)
                        for et in range(ET):
                            if not start:
                                dve.wait_ge(s_state, ET * n2 + et - (ET - 1))
                            dve.tensor_tensor(drive[:, et], du[:, p * ET + et].unsqueeze(1).to_broadcast((P, 2, T)),
                                              ps[:, 2 + 2 * par:4 + 2 * par], ALU.mult).then_inc(s_drive, 1)
                        for et in range(ET):
                            n = ET * n2 + et
                            dve.wait_ge(s_drive, n + 1)
                            dve.wait_ge(s_decay, 2 * n + 2)
                            if not start:
                                dve.wait_ge(s_prod, n - (ET - 1))
                            dve.tensor_tensor_scan(state[:, et].rearrange("p j t -> p (j t)"),
                                                   decay[:, et].rearrange("p j b l -> p (j b l)"),
                                                   drive[:, et].rearrange("p j t -> p (j t)"),
                                                   0.0, ALU.mult, ALU.add).then_inc(s_state, 1)
                        if p and isinstance(i, int) and i == 0 and par == 0:
                            gate_y(p - 1)
                over_state_pairs(dve, p, scans)
            dve.wait_ge(s_small, 48)
            dve.tensor_copy(wg_hi[:], wg[:]).then_inc(s_wg, 1)
            dve.wait_ge(s_wg, 1)
            dve.tensor_tensor(wg_lo[:], wg[:], wg_hi[:].bitcast(F32), ALU.subtract).then_inc(s_wg, 1)
            gate_y(PAIRS - 1)

            for b in range(B):
                dve.wait_ge(s_yt, b + 1)
                x1 = xs[:, 2 * b:2 * b + 2].rearrange("p t h -> p (t h)")
                dve.wait_ge(s_ln1, 3 * NT + RS + 2)
                dve.wait_ge(s_zt, NT)
                dve.tensor_tensor(x1, x1, ps[:, 2 + b], ALU.add).then_inc(s_x1, 1)
            for t in range(NT):
                dve.wait_ge(s_x1, t // 2 + 1)
                dve.bn_stats(stats2[:, t], xs[:, t]).then_inc(s_ln2, 1)
            for t in range(NT):
                dve.wait_ge(s_ln2, t + 1)
                dve.bn_aggr(mv2[:, t], stats2[:, t]).then_inc(s_ln2, 1)
            inverse_root(rstd2, mv2, inv_var2, s_ln2, 2)
            dve.wait_ge(s_prod, PAIRS * N2 * ET)
            for t in range(NT):
                dve.tensor_scalar(xn[:, t], xs[:, t], mv2[:, t, 0:1], rstd2[:, t:t + 1], ALU.subtract, ALU.mult).then_inc(s_xn, 1)
            for n in range(HK * TG):
                dve.wait_ge(s_xhi, n + 1)
                cols = slice(n % TG * T, (n % TG + 1) * T)
                dve.tensor_tensor(xt_lo[:, n // TG, cols], ps[:, n], xt_hi[:, n // TG, cols].bitcast(F32),
                                  ALU.subtract).then_inc(s_xlo, 1)

            over_e = lambda a: a.unsqueeze(2).to_broadcast((P, NT, E))
            steps = [0]

            def step(instruction):
                steps[0] += 1
                instruction.then_inc(s_rtv, 1)
                dve.wait_ge(s_rtv, steps[0])

            dve.wait_ge(s_rta, 1)
            step(dve.tensor_reduce(lg_max[:], lg_tanh[:], AX_X, ALU.max))
            step(dve.tensor_tensor(lg_exp[:], lg_tanh[:], over_e(lg_max[:]), ALU.subtract))
            dve.wait_ge(s_rta, 2)
            step(dve.tensor_reduce(lg_sum[:], lg_exp[:], AX_X, ALU.add))
            step(dve.reciprocal(lg_sum[:], lg_sum[:]))
            dve.wait_ge(s_pad, 6)
            step(dve.tensor_tensor(probs[:, :, 0:E], lg_exp[:], over_e(lg_sum[:]), ALU.mult))
            for t in range(NT):
                dve.max(top8[:, t], probs[:, t, 0:E]).then_inc(s_rtv, 1)
            steps[0] += NT
            dve.wait_ge(s_rtv, steps[0])
            step(dve.tensor_copy(chosen[:, :, 0:TOPK], top8[:, :, 0:TOPK]))
            for t in range(NT):
                dve.match_replace(others[:, t], chosen[:, t], probs[:, t], 0.0).then_inc(s_rtv, 1)
            steps[0] += NT
            dve.wait_ge(s_rtv, steps[0])
            step(dve.tensor_tensor(weight[:], probs[:, :, 0:E], others[:, :, 0:E], ALU.subtract))

            weight_q = weight[:].rearrange("p t (i j) -> p t i j", j=2)

            def add_expert(i, j, g):
                dve.wait_ge(s_down, UB * i + (j * UE + (g + 1) * IT))
                for t in range(TT):
                    a = g * TT + t
                    dve.scalar_tensor_tensor(xs[:, a], ps[:, 4 + 2 * g + t // 2, t % 2 * H:(t % 2 + 1) * H],
                                             weight_q[:, a, i, j:j + 1], xs[:, a], ALU.mult, ALU.add).then_inc(s_acc, 1)

            def expert_pair(i, first, last):
                for v in range(UB):
                    n = UB * i + v
                    dve.wait_ge(s_gt, n + 1)
                    if not first or v >= 2:
                        dve.wait_ge(s_hid, n - 1)
                    dve.scalar_tensor_tensor(g_silu2[:, v % 2], g_tanh[:, v % 2], 1.0, ps[:, v % 2 * 2], ALU.add,
                                             ALU.mult).then_inc(s_gs, 1)
                    dve.wait_ge(s_gs, n + 1)
                    dve.wait_ge(s_up, n + 1)
                    if not first or v >= 2:
                        dve.wait_ge(s_hlo, n - 1)
                    dve.scalar_tensor_tensor(hid[:, v % 2], g_silu2[:, v % 2], 0.5, ps[:, v % 2 * 2 + 1], ALU.mult,
                                             ALU.mult).then_inc(s_hid, 1)
                    if v == 2 and not first:
                        add_expert(i - 1, 1, TG - 1)
                    if v in (6, 10, 14):
                        add_expert(i, (v - 3) // UE, (v - 3) // IT % TG)

            over_expert_pairs(dve, expert_pair)
            add_expert(E // 2 - 1, 1, TG - 1)


def kernel(x, ctx_1024, L0_xattn_in_proj_w, L0_xattn_conv_w, L0_xattn_conv_b, L0_xattn_x_proj_w, L0_xattn_dt_proj_w,
           L0_xattn_dt_proj_b, L0_xattn_A_log, L0_xattn_D, L0_ffn_w_gate, L0_ffn_w1, L0_ffn_w3, L0_ffn_w2):
    import numpy as np
    import concourse.bacc as bacc
    from concourse.bass_utils import run_bass_kernel_spmd

    x_proj_t = np.transpose(L0_xattn_x_proj_w)
    dt_rank = L0_xattn_dt_proj_w.shape[1]
    given = {
        "x": x, "ctx_t": np.transpose(ctx_1024, (2, 0, 1)), "in_proj_t": np.transpose(L0_xattn_in_proj_w),
        "conv_w_t": np.transpose(L0_xattn_conv_w),
        "channel_rows": np.concatenate([L0_xattn_conv_b[:, None], L0_xattn_dt_proj_b[:, None],
                                        L0_xattn_D[:, None], L0_xattn_A_log], axis=1),
        "x_proj_rows": np.concatenate([x_proj_t[:, dt_rank:]] * 3 + [x_proj_t[:, :dt_rank]], axis=1),
        "dt_proj_t": np.transpose(L0_xattn_dt_proj_w),
        "w_gate": L0_ffn_w_gate, "w1": L0_ffn_w1, "w3": L0_ffn_w3, "w2": L0_ffn_w2,
    }
    nc = bacc.Bacc("TRN2", target_bir_lowering=False, num_devices=1)
    arrays, args = {}, {}
    for name, a in given.items():
        a = np.ascontiguousarray(a)
        arrays[f"in_{name}"] = a
        args[name] = nc.dram_tensor(f"in_{name}", a.shape, mybir.dt.from_np(a.dtype), kind="ExternalInput").ap()
    out = nc.dram_tensor("out", x.shape, F32, kind="ExternalOutput").ap()
    xattn_ffn(nc, **args, out=out)
    r = run_bass_kernel_spmd(nc, [arrays], core_ids=[0])
    return r.results[0]["out"]
```

```python
from contextlib import ExitStack

import concourse.bass as bass
from concourse import mybir

P = 128
ALU = mybir.AluOpType
ACT = mybir.ActivationFunctionType
F32 = mybir.dt.float32
F32R = mybir.dt.float32r
BF16 = mybir.dt.bfloat16
AX_X = mybir.AxisListType.X

EPS = 1e-5
SOFTCAP = 30.0
TOPK = 2
RS = 6


def xattn_ffn(nc, x, ctx_t, in_proj_t, conv_w_t, channel_rows, x_proj_rows, dt_proj_t, w_gate, w1, w3, w2, out):
    DM, B, L = ctx_t.shape
    DI = in_proj_t.shape[1]
    TAPS = conv_w_t.shape[0]
    DR = dt_proj_t.shape[0]
    DS = channel_rows.shape[1] - 3
    E, H, I = w1.shape
    assert DM == P and DI == L == H == 2 * P and DS == 16
    PAD = TAPS - 1
    ET = DI // P
    PAIRS = B // 2
    T = 2 * L
    NT = B * L // P
    N2 = DS // 2
    BCR = 2 * DS
    DT0 = 3 * BCR
    HK = H // P
    IT = I // P
    TG = B * L // T
    TT = T // P
    UE = TG * IT
    UB = 2 * UE
    WCOLS = 2 * HK * I + IT * H
    W3_AT, W2_AT = HK * I, 2 * HK * I

    with ExitStack() as ctx:
        def sb(name, shape, dt=F32):
            return ctx.enter_context(nc.sbuf_tensor(name, shape, dt))

        def sem(name):
            return ctx.enter_context(nc.semaphore(name))

        ctx_pad = sb("ctx_pad", [P, B, L + PAD])
        inw = sb("inw", [P, DI])
        tapw = sb("tapw", [P, TAPS, DI])
        channel = sb("channel", [P, ET, 3 + DS])
        conv_bias, dt_bias, dskip, alog = channel[:, :, 0], channel[:, :, 1], channel[:, :, 2], channel[:, :, 3:]
        half_conv_bias = sb("half_conv_bias", [P, ET])
        xpw = sb("xpw", [P, ET, DT0 + DR])
        dtw = sb("dtw", [P, DI])
        exp_alog = sb("exp_alog", [P, ET, DS])
        neg_a = sb("neg_a", [P, ET, DS])
        diag_d = sb("diag_d", [P, ET, P])
        ident = sb("ident", [P, P])
        ident_bc = sb("ident_bc", [P, BCR], BF16)
        select = sb("select", [P, BCR, P], BF16)
        xs = sb("xs", [P, NT, H])
        wg = sb("wg", [P, HK, E])
        wg_hi = sb("wg_hi", [P, HK, P], F32R)
        wg_lo = sb("wg_lo", [P, HK, P], F32R)

        tanh_t = sb("tanh_t", [P, PAIRS * ET, T])
        u = sb("u", [P, PAIRS * ET, T])
        convw = u[:, 0:2].rearrange("p n (k e) -> p (n k) e", e=DI)
        bc_round = sb("bc_round", [P, T], BF16)
        bc_mid = sb("bc_mid", [P, T], BF16)
        bc = sb("bc", [P, PAIRS, T], BF16)
        dt_lo = sb("dt_lo", [P, PAIRS, T])
        delta = sb("delta", [P, PAIRS * ET, 2, L])
        du = sb("du", [P, PAIRS * ET, T])

        stats = sb("stats", [P, NT, 6])
        mv = sb("mv", [P, NT, 2])
        rstd = sb("rstd", [P, NT])
        inv_var = sb("inv_var", [P, NT])
        half_rstd = sb("half_rstd", [P, NT])
        neg_half_mr = sb("neg_half_mr", [P, NT])
        zt = sb("zt", [P, NT, L])

        decay = sb("decay", [P, ET, 2, 2, L])
        drive = sb("drive", [P, ET, 2, T])
        state = sb("state", [P, ET, 2, T])
        c_rows = sb("c_rows", [P, 2, 2, T])
        prod = sb("prod", [P, ET, 2, T])
        w_raw = sb("w_raw", [P, WCOLS])
        scratch = w_raw[:].rearrange("p (n t) -> p n t", t=T)
        sp_exp = (state[:, 0], scratch[:, 0:2])
        sp_ln = (state[:, 1], scratch[:, 2:4])
        sp_max = (drive[:, 0], scratch[:, 4:6])
        half_t = prod[:].rearrange("p a b t -> p (a b) t")
        bc_rest = c_rows[:, :, 1]
        yg = tanh_t[:].rearrange("p n (b l) -> p n b l", b=2)

        stats2 = sb("stats2", [P, NT, 6])
        mv2 = sb("mv2", [P, NT, 2])
        rstd2 = sb("rstd2", [P, NT])
        inv_var2 = sb("inv_var2", [P, NT])
        xn = decay[:].rearrange("p a b c h -> p (a b c) h")
        xt_hi = sb("xt_hi", [P, HK, B * L], F32R)
        xt_lo = sb("xt_lo", [P, HK, B * L], F32R)
        lg_cols = u[:, 0:TG]
        lg_max = sb("lg_max", [P, NT])
        lg_exp = sb("lg_exp", [P, NT, E])
        lg_sum = sb("lg_sum", [P, NT])
        probs = sb("probs", [P, NT, E + 8 - TOPK])
        top8 = sb("top8", [P, NT, 8])
        chosen = sb("chosen", [P, NT, 8])
        others = sb("others", [P, NT, E + 8 - TOPK])
        weight = sb("weight", [P, NT, E])

        w_hi = sb("w_hi", [P, 2, WCOLS], F32R)
        w_lo = sb("w_lo", [P, 2, WCOLS], F32R)
        g_tanh, g_silu2 = state[:, 0], state[:, 1]
        hid = drive[:, 0]
        hid_hi = sb("hid_hi", [P, 2, T], F32R)
        hid_lo = sb("hid_lo", [P, 2, T], F32R)

        ps = ctx.enter_context(nc.psum_tensor("ps", [P, 8, T], F32))
        def gate_bank(v):
            return 2 - 2 * (v % 2)

        s_small = sem("small_landed")
        s_vec = sem("vectors_landed")
        s_ctx = sem("ctx_of_pair_0_landed")
        s_ctx1 = sem("ctx_of_pair_1_landed")
        s_x = sem("x_landed")
        s_raw = sem("raw_landed")
        s_inw = sem("in_proj_landed")
        s_out = sem("out_stored")
        s_const = sem("constants_built")
        s_pad = sem("pads_cleared")
        s_tap = sem("tap_weights_ready")
        s_const_v = sem("vector_constants_ready")
        s_alog = sem("exp_alog_ready")
        s_conv = sem("conv_done")
        s_tanh = sem("conv_tanh_done")
        s_half = sem("conv_half_done")
        s_selm = sem("select_ready")
        s_u = sem("u_done")
        s_xp = sem("x_proj_done")
        s_bca = sem("bc_rounded")
        s_bcv = sem("bc_parts_vector")
        s_dtlo = sem("dt_lo_ready")
        s_dt = sem("dt_proj_done")
        s_spa = sem("softplus_scalar_steps")
        s_spv = sem("softplus_vector_steps")
        s_du = sem("du_ready")
        s_ln1 = sem("ln1_steps")
        s_root = sem("variance_root_done")
        s_zt = sem("z_tanh_done")
        s_zs = sem("z_tanh_scaled")
        s_gz = sem("gated_z_ready")
        s_rows = sem("bc_rows_broadcast")
        s_crow = sem("c_rows_copied")
        s_decay = sem("decay_ready")
        s_drive = sem("drive_ready")
        s_state = sem("state_ready")
        s_prod = sem("prod_ready")
        s_sum = sem("prod_summed")
        s_open = sem("y_opened")
        s_yg = sem("yg_ready")
        s_yt = sem("y_turned")
        s_x1 = sem("x1_ready")
        s_ln2 = sem("ln2_steps")
        s_xn = sem("xn_ready")
        s_xt = sem("xn_turned")
        s_xhi = sem("xt_hi_ready")
        s_xlo = sem("xt_lo_ready")
        s_wgz = sem("gate_weight_pads_cleared")
        s_lgt = sem("logits_in_token_rows")
        s_lg = sem("logits_done")
        s_rta = sem("router_scalar_steps")
        s_rtv = sem("router_vector_steps")
        s_whi = sem("w_hi_ready")
        s_wlo = sem("w_lo_ready")
        s_wg = sem("gate_weights_split")
        s_gate = sem("gate_done")
        s_up = sem("up_done")
        s_gt = sem("gate_tanh_done")
        s_gs = sem("gate_silu_done")
        s_hid = sem("hid_done")
        s_hhi = sem("hid_hi_done")
        s_hlo = sem("hid_lo_done")
        s_down = sem("down_unit_done")
        s_acc = sem("down_added")

        x_proj_bank, dt_bank = (6, 5), (0, 4)

        x_rows = x.rearrange("b (t p) h -> p (b t) h", p=P)
        out_rows = out.rearrange("b (t p) h -> p (b t) h", p=P)
        w1_d = w1.rearrange("e (k p) i -> e p k i", p=P)
        w3_d = w3.rearrange("e (k p) i -> e p k i", p=P)
        w2_d = w2.rearrange("e (k p) h -> e p k h", p=P)

        block = ctx.enter_context(nc.Block())

        @block.sync
        def _(sp):
            sp.dma_start(inw[:], in_proj_t).then_inc(s_inw, 16)
            sp.dma_start(convw, conv_w_t.rearrange("(o k) e -> o k e", o=1).to_broadcast((P, TAPS, DI))).then_inc(s_inw, 16)
            sp.dma_start(ctx_pad[:, 2:4, PAD:], ctx_t[:, 2:4]).then_inc(s_ctx1, 16)
            sp.dma_start(xpw[:], x_proj_rows.rearrange("(k p) c -> p k c", p=P)).then_inc(s_small, 16)
            sp.dma_start(dtw[DT0:DT0 + DR, :], dt_proj_t).then_inc(s_small, 16)
            sp.dma_start(wg[:], w_gate.rearrange("(k p) e -> p k e", p=P)).then_inc(s_small, 16)

            def load_expert(e):
                for at, w, k in ((0, w1_d, HK), (W3_AT, w3_d, HK), (W2_AT, w2_d, IT)):
                    sp.dma_start(w_raw[:, at:at + WCOLS // 3].rearrange("p (k i) -> p k i", k=k),
                                 w[e].rearrange("o p k i -> (o p) k i")).then_inc(s_raw, 16)

            sp.wait_ge(s_du, PAIRS * ET)
            load_expert(slice(0, 1))
            with sp.Fori(0, E - 1) as e:
                sp.wait_ge(s_whi, IT * e + IT)
                sp.wait_ge(s_wlo, IT * e + IT)
                load_expert(bass.ds(e + 1, 1))
            for g in range(TG):
                sp.wait_ge(s_acc, (E - 1) * TG * TT + (g + 1) * TT)
                sp.dma_start(out_rows[:, g * TT:(g + 1) * TT], xs[:, g * TT:(g + 1) * TT]).then_inc(s_out, 16)
            sp.wait_ge(s_out, 16 * TG)

        def over_state_pairs(engine, p, body):
            body(0)
            with engine.Fori(1, N2 // 2 - 1) as i:
                body(i)
            body(N2 // 2 - 1)

        def over_expert_pairs(engine, body):
            body(0, True, False)
            with engine.Fori(1, E // 2 - 1) as i:
                body(i, False, False)
            body(E // 2 - 1, False, True)

        @block.gpsimd
        def _(pool):
            pool.memset(ctx_pad[:, :, 0:PAD], 0.0).then_inc(s_pad, 1)
            pool.memset(ident_bc[:], 0.0).then_inc(s_pad, 1)
            pool.memset(ident[:], 0.0).then_inc(s_pad, 1)
            pool.wait_ge(s_pad, 2)
            for copy in range(3):
                pool.affine_select(out=ident_bc[:], in_=ident_bc[:], compare_op=ALU.not_equal, fill=1.0,
                                   base=-copy * BCR, pattern=[[-1, BCR]], channel_multiplier=1).then_inc(s_const, 1)
                pool.wait_ge(s_const, copy + 1)
            pool.wait_ge(s_pad, 3)
            pool.affine_select(out=ident[:], in_=ident[:], compare_op=ALU.not_equal, fill=1.0, base=0,
                               pattern=[[-1, P]], channel_multiplier=1).then_inc(s_const, 1)
            pool.tensor_copy(select[:], ident_bc[:].unsqueeze(2).to_broadcast((P, BCR, P))).then_inc(s_selm, 1)
            pool.memset(decay[:, :, :, :, 0:1].rearrange("p a b c o -> p (a b c) o"), 0.0).then_inc(s_pad, 1)
            pool.memset(probs[:], -1.0).then_inc(s_pad, 1)
            pool.memset(chosen[:], -1.0).then_inc(s_pad, 1)
            pool.memset(wg_hi[:].bitcast(F32), 0.0).then_inc(s_wgz, 1)
            pool.memset(wg_lo[:].bitcast(F32), 0.0).then_inc(s_wgz, 1)

            pool.wait_ge(s_u, PAIRS * ET)
            for p in range(PAIRS):
                def c_products(i):
                    for par in range(2):
                        n2 = 2 * i + (p * N2 + par)
                        for et in range(ET):
                            n = ET * n2 + et
                            pool.wait_ge(s_state, n + 1)
                            pool.wait_ge(s_crow, n2 + 1)
                            if not (p == 0 and isinstance(i, int) and i == 0 and par == 0):
                                pool.wait_ge(s_sum, n - (ET - 1))
                            pool.tensor_tensor(prod[:, et], state[:, et], c_rows[:, par], ALU.mult).then_inc(s_prod, 1)
                over_state_pairs(pool, p, c_products)

            def split_low(e, j, q):
                n = WCOLS // IT
                pool.wait_ge(s_whi, IT * e + (q + 1))
                pool.tensor_tensor(w_lo[:, j, q * n:(q + 1) * n], w_raw[:, q * n:(q + 1) * n],
                                   w_hi[:, j, q * n:(q + 1) * n].bitcast(F32), ALU.subtract).then_inc(s_wlo, 1)

            for q in range(IT):
                split_low(0, 0, q)

            def expert_pair(i, first, last):
                for v in range(UB):
                    n = UB * i + v
                    pool.wait_ge(s_hhi, n + 1)
                    if not first or v >= 2:
                        pool.wait_ge(s_down, n - 1)
                    pool.tensor_tensor(hid_lo[:, v % 2], hid[:, v % 2], hid_hi[:, v % 2].bitcast(F32),
                                       ALU.subtract).then_inc(s_hlo, 1)
                    if 2 <= v % UE < 2 + IT and (v < UE or not last):
                        split_low(2 * i + (1 + v // UE), 1 - v // UE, v % UE - 2)

            over_expert_pairs(pool, expert_pair)

        @block.scalar
        def _(act):
            act.dma_start(ctx_pad[:, 0:2, PAD:], ctx_t[:, 0:2]).then_inc(s_ctx, 16)
            act.dma_start(channel[:], channel_rows.rearrange("(k p) c -> p k c", p=P)).then_inc(s_vec, 16)
            for g in range(TG):
                act.dma_start(xs[:, g * TT:(g + 1) * TT], x_rows[:, g * TT:(g + 1) * TT]).then_inc(s_x, 16)
            act.wait_ge(s_vec, 16)
            act.activation(exp_alog[:], alog, ACT.Exp).then_inc(s_alog, 1)

            act.wait_ge(s_const_v, 1)

            def conv_halves(n):
                bias = half_conv_bias[:, n % ET:n % ET + 1]
                act.wait_ge(s_conv, n + 1)
                act.activation(tanh_t[:, n], ps[:, 2 + n], ACT.Tanh, scale=0.5, bias=bias).then_inc(s_tanh, 1)
                act.activation(half_t[:, n], ps[:, 2 + n], ACT.Identity, scale=0.5, bias=bias).then_inc(s_half, 1)

            def z_tanh(tiles):
                for t in tiles:
                    act.activation(zt[:, t], xs[:, t], ACT.Tanh, scale=half_rstd[:, t:t + 1],
                                   bias=neg_half_mr[:, t:t + 1]).then_inc(s_zt, 1)

            def z_scale(tiles):
                for t in tiles:
                    act.wait_ge(s_zt, t + 1)
                    act.activation(zt[:, t], zt[:, t], ACT.Identity, scale=rstd[:, t:t + 1], bias=rstd[:, t:t + 1]).then_inc(s_zs, 1)

            def round_bc(p):
                bank = x_proj_bank[p]
                act.wait_ge(s_xp, p + 1)
                act.activation(dt_lo[DT0:DT0 + DR, p], ps[DT0:DT0 + DR, bank], ACT.Copy).then_inc(s_dtlo, 1)
                if p:
                    act.wait_ge(s_bcv, 5 * p)
                act.activation(bc_round[0:DT0], ps[0:DT0, bank], ACT.Copy).then_inc(s_bca, 1)

            def softplus_in(p):
                for et in range(ET):
                    act.wait_ge(s_dt, p * ET + et + 1)
                    act.activation(sp_exp[p][:, et], ps[:, dt_bank[p] + et], ACT.Abs, bias=dt_bias[:, et:et + 1]).then_inc(s_spa, 1)
                    act.activation(sp_max[p][:, et], ps[:, dt_bank[p] + et], ACT.Relu, bias=dt_bias[:, et:et + 1]).then_inc(s_spa, 1)

            def softplus_exp(p):
                for et in range(ET):
                    act.wait_ge(s_spa, 8 * p + 2 * et + 1)
                    act.activation(sp_exp[p][:, et], sp_exp[p][:, et], ACT.Exp, scale=-1.0).then_inc(s_spa, 1)

            def softplus_ln(p):
                for et in range(ET):
                    act.wait_ge(s_spa, 8 * p + 2 * ET + et + 1)
                    act.activation(sp_ln[p][:, et], sp_exp[p][:, et], ACT.Ln, bias=1.0).then_inc(s_spa, 1)

            conv_halves(0)
            conv_halves(1)
            act.wait_ge(s_ln1, 2 * NT + 2)
            act.activation(rstd[:], inv_var[:], ACT.Sqrt).then_inc(s_root, 1)
            conv_halves(2)
            round_bc(0)
            softplus_in(0)
            softplus_exp(0)
            softplus_ln(0)
            conv_halves(3)

            neg_a_q = neg_a[:].rearrange("p k (i q) -> p k i q", q=4)
            act.wait_ge(s_pad, 4)
            act.wait_ge(s_const_v, 4)
            def split_high(j, q):
                n = WCOLS // IT
                act.activation(w_hi[:, j, q * n:(q + 1) * n], w_raw[:, q * n:(q + 1) * n], ACT.Copy).then_inc(s_whi, 1)

            for p in range(PAIRS):
                def decays(i):
                    for par in range(2):
                        n2 = 2 * i + (p * N2 + par)
                        start = p == 0 and isinstance(i, int) and i == 0
                        act.wait_ge(s_rows, n2 + 1)
                        if start and par:
                            act.wait_ge(s_bcv, 5 * PAIRS)
                        if not start:
                            act.wait_ge(s_prod, ET * n2 - ET)
                        act.activation(c_rows[:, par], ps[:, 6:8], ACT.Copy).then_inc(s_crow, 1)
                        for et in range(ET):
                            if not (start and par == 0):
                                act.wait_ge(s_state, ET * n2 + et - (ET - 1))
                            if isinstance(i, int) and i == 0 and par == 0:
                                act.wait_ge(s_spv, 4 * ET * p + (3 * ET + et + 1))
                            for j in range(2):
                                act.activation(decay[:, et, j, :, 1:], delta[:, p * ET + et, :, 1:], ACT.Exp,
                                               scale=neg_a_q[:, et, i, 2 * par + j:2 * par + j + 1]).then_inc(s_decay, 1)
                        if start and par == 0:
                            round_bc(1)
                            softplus_in(1)
                        if start and par == 1:
                            softplus_exp(1)
                            act.wait_ge(s_ln1, 2 * NT + RS + 2)
                            z_tanh(range(0, NT // 2))
                        if p == 0 and isinstance(i, int) and i == N2 // 2 - 1:
                            if par == 0:
                                softplus_ln(1)
                            else:
                                z_scale(range(0, NT // 2))
                        if p == PAIRS - 1 and isinstance(i, int) and i == N2 // 2 - 1:
                            if par == 0:
                                act.wait_ge(s_raw, 48)
                            split_high(0, 2 * par)
                            split_high(0, 2 * par + 1)
                over_state_pairs(act, p, decays)

            def second_root(g):
                act.wait_ge(s_ln2, (2 * TT + RS) * g + 2 * TT + 2)
                act.activation(rstd2[:, g * TT:(g + 1) * TT], inv_var2[:, g * TT:(g + 1) * TT], ACT.Sqrt).then_inc(s_root, 1)

            def columns_high(g):
                for k in range(HK):
                    act.wait_ge(s_xt, HK * g + k + 1)
                    act.activation(xt_hi[:, k, g * T:(g + 1) * T], ps[:, 4 + HK * g + k], ACT.Copy).then_inc(s_xhi, 1)

            z_tanh(range(NT // 2, NT))
            second_root(0)
            z_scale(range(NT // 2, NT))
            columns_high(0)

            def expert_pair(i, first, last):
                for v in range(UB):
                    n = UB * i + v
                    act.wait_ge(s_gate, n + 1)
                    if not first or v >= 2:
                        act.wait_ge(s_gs, n - 1)
                    act.activation(g_tanh[:, v % 2], ps[:, gate_bank(v)], ACT.Tanh, scale=0.5).then_inc(s_gt, 1)
                    if first and v == 1:
                        second_root(1)
                    if first and v == 2:
                        columns_high(1)
                    if first and v == 3:
                        for g in range(TG):
                            act.wait_ge(s_lg, g + 1)
                            act.activation(lg_cols[0:E, g], ps[0:E, 6 + g], ACT.Tanh, scale=1.0 / SOFTCAP).then_inc(s_rta, 1)
                    if 2 <= v % UE < 2 + IT and (v < UE or not last):
                        if v % UE == 2:
                            act.wait_ge(s_raw, 96 * i + (96 + 48 * (v // UE)))
                            if not first or v >= UE:
                                act.wait_ge(s_down, UB * i + v // UE * UE)
                        split_high(1 - v // UE, v % UE - 2)
                    act.wait_ge(s_hid, n + 1)
                    if not first or v >= 2:
                        act.wait_ge(s_down, n - 1)
                    act.activation(hid_hi[:, v % 2], hid[:, v % 2], ACT.Copy).then_inc(s_hhi, 1)
                    if first and v == 3:
                        act.wait_ge(s_rtv, 2)
                        act.activation(lg_exp[:], lg_exp[:], ACT.Exp, scale=SOFTCAP).then_inc(s_rta, 1)

            over_expert_pairs(act, expert_pair)

        @block.tensor
        def _(pe):
            pe.wait_ge(s_tap, 1)
            pe.wait_ge(s_pad, 1)
            pe.wait_ge(s_ctx, 16)

            def convolution(n):
                p, et = n // ET, n % ET
                for k in range(TAPS):
                    mm = pe.matmul(ps[:, 2 + n].rearrange("p (b l) -> p b l", b=2), tapw[:, k, et * P:(et + 1) * P],
                                   ctx_pad[:, 2 * p:2 * p + 2, k:k + L], start=(k == 0), stop=(k == TAPS - 1))
                mm.then_inc(s_conv, 1)

            def x_proj(p):
                if p:
                    pe.wait_ge(s_half, PAIRS * ET)
                for k in range(ET):
                    pe.wait_ge(s_u, p * ET + k + 1)
                    mm = pe.matmul(ps[0:DT0 + DR, x_proj_bank[p]], xpw[:, k, :], u[:, p * ET + k], start=(k == 0),
                                   stop=(k == ET - 1))
                mm.then_inc(s_xp, 1)

            def dt_proj(p):
                pe.wait_ge(s_dtlo, p + 1)
                for et in range(ET):
                    if p and et:
                        pe.wait_ge(s_bcv, 5 * p + 1)
                    pe.matmul(ps[:, dt_bank[p] + et], dtw[DT0:DT0 + DR, et * P:(et + 1) * P], dt_lo[DT0:DT0 + DR, p],
                              start=True, stop=True).then_inc(s_dt, 1)

            convolution(0)
            pe.wait_ge(s_tap, 2)
            convolution(1)
            pe.wait_ge(s_ctx1, 16)
            convolution(2)
            pe.wait_ge(s_small, 48)
            x_proj(0)
            dt_proj(0)
            convolution(3)

            def broadcast_rows(p, i, par):
                for at, bank in ((0, 2 + 2 * par), (DS, 6)):
                    for j in range(2):
                        row = 4 * i + (at + 2 * par + j)
                        sel = select[0:DT0, row, :] if isinstance(row, int) else \
                            select[0:DT0, bass.ds(row, 1), :].rearrange("p o m -> p (o m)")
                        mm = pe.matmul(ps[:, bank + j], sel, bc[0:DT0, p], start=True, stop=True)
                mm.then_inc(s_rows, 1)

            pe.wait_ge(s_selm, 1)
            pe.wait_ge(s_bcv, 5)
            broadcast_rows(0, 0, 0)
            pe.wait_ge(s_const_v, 3)
            pe.wait_ge(s_spa, 2 * ET)
            def add_skip(p, opens):
                for et in range(ET):
                    pe.matmul(ps[:, et], diag_d[:, et], u[:, p * ET + et], start=opens, stop=False, skip_group_check=True)

            def turn_y(p):
                pe.wait_ge(s_yg, ET * (p + 1))
                for t in range(TT):
                    b, half = t // 2, t % 2
                    for et in range(ET):
                        mm = pe.transpose(ps[:, (2, 6)[p] + b, half * DI + et * P:half * DI + (et + 1) * P],
                                          yg[:, p * ET + et, b, half * P:(half + 1) * P], ident[:])
                    if half:
                        mm.then_inc(s_yt, 1)

            for p in range(PAIRS):
                if p == 0:
                    add_skip(p, True)
                if p == 0:
                    x_proj(1)
                    dt_proj(1)
                    pe.wait_ge(s_spa, 6 * ET)
                    pe.wait_ge(s_bcv, 5 * PAIRS)
                    pe.wait_ge(s_crow, 1)
                    broadcast_rows(0, 0, 1)

                def sum_products(i, par, n2):
                    opens = p > 0 and isinstance(i, int) and i == 0 and par == 0
                    final = isinstance(i, int) and i == N2 // 2 - 1 and par == 1
                    if opens:
                        pe.wait_ge(s_yg, ET * p)
                    for et in range(ET):
                        pe.wait_ge(s_prod, ET * n2 + (et + 1))
                        for j in range(2):
                            mm = pe.matmul(ps[:, et], ident[:], prod[:, et, j], start=opens and j == 0,
                                           stop=final and j == 1, skip_group_check=True)
                        mm.then_inc(s_sum, 1)

                def sums(i):
                    for par in range(2):
                        n2 = 2 * i + (p * N2 + par)
                        last = isinstance(i, int) and i == N2 // 2 - 1
                        start = p == 0 and isinstance(i, int) and i == 0 and par == 0
                        if start:
                            sum_products(i, par, n2)
                        if last and p == PAIRS - 1:
                            if par == 0:
                                pe.wait_ge(s_drive, ET * n2 + ET)
                                turn_y(0)
                            else:
                                add_skip(p, False)
                        else:
                            pe.wait_ge(s_drive, ET * n2 + ET)
                            pe.wait_ge(s_crow, n2 + 2)
                            if last:
                                broadcast_rows(p + 1, 0, par)
                            else:
                                broadcast_rows(p, i + 1, par)
                        if not start:
                            sum_products(i, par, n2)
                over_state_pairs(pe, p, sums)

            def turn_xn(g):
                pe.wait_ge(s_xn, TT * (g + 1))
                for k in range(HK):
                    for t in range(TT):
                        mm = pe.transpose(ps[:, 4 + HK * g + k, t * P:(t + 1) * P], xn[:, g * TT + t, k * P:(k + 1) * P], ident[:])
                    mm.then_inc(s_xt, 1)

            def logits():
                pe.wait_ge(s_wg, 2)
                pe.wait_ge(s_xhi, HK * TG)
                pe.wait_ge(s_xlo, HK * TG)
                for g in range(TG):
                    for k in range(HK):
                        for m, (wa, xa) in enumerate(((wg_hi, xt_hi), (wg_hi, xt_lo), (wg_lo, xt_hi), (wg_lo, xt_lo))):
                            mm = pe.matmul(ps[:, 6 + g], wa[:, k, :], xa[:, k, g * T:(g + 1) * T],
                                           start=(k == 0 and m == 0), stop=(k == HK - 1 and m == 3))
                    mm.then_inc(s_lg, 1)

            def turn_logits():
                pe.wait_ge(s_rta, TG)
                for t in range(NT):
                    mm = pe.transpose(ps[:, 6, t * E:(t + 1) * E], lg_cols[0:E, t // TT, t % TT * P:(t % TT + 1) * P],
                                      ident[0:E, 0:E])
                mm.then_inc(s_lgt, 1)

            w1_of = lambda w, j, k, it: w[:, j, k * I + it * P:k * I + (it + 1) * P]
            w3_of = lambda w, j, k, it: w[:, j, W3_AT + k * I + it * P:W3_AT + k * I + (it + 1) * P]
            w2_of = lambda w, j, it: w[:, j, W2_AT + it * H:W2_AT + (it + 1) * H]

            def gate_up(i, v, first):
                n = UB * i + v
                j, g, it, par = v // UE % 2, v // IT % TG, v % IT, v % 2
                if v % UE == 0:
                    pe.wait_ge(s_wlo, 2 * IT * i + (v // UE * IT + IT - 1))
                for made, of, bank, freed in ((s_gate, w1_of, gate_bank(par), s_gs), (s_up, w3_of, gate_bank(par) + 1, s_hid)):
                    if not (first and v < 2):
                        pe.wait_ge(freed, n - 1)
                    for k in range(HK):
                        for m, (wa, xa) in enumerate(((w_hi, xt_hi), (w_hi, xt_lo), (w_lo, xt_hi))):
                            mm = pe.matmul(ps[:, bank], of(wa, j, k, it), xa[:, k, g * T:(g + 1) * T],
                                           start=(k == 0 and m == 0), stop=(k == HK - 1 and m == 2))
                    mm.then_inc(made, 1)

            def down(i, v, first):
                n = UB * i + v
                j, g, it, par = v // UE, v // IT % TG, v % IT, v % 2
                if v % UE == 0:
                    pe.wait_ge(s_wlo, 2 * IT * i + (j * IT + IT))
                if it == 0 and not (first and j == 0):
                    pe.wait_ge(s_acc, 2 * TG * TT * i + ((j - 1) * TG * TT + (g + 1) * TT))
                pe.wait_ge(s_hhi, n + 1)
                pe.wait_ge(s_hlo, n + 1)
                for t in range(TT):
                    for m, (ha, wa) in enumerate(((hid_hi, w_hi), (hid_hi, w_lo), (hid_lo, w_hi))):
                        mm = pe.matmul(ps[:, 4 + 2 * g + t // 2, t % 2 * H:(t % 2 + 1) * H], ha[:, par, t * P:(t + 1) * P],
                                       w2_of(wa, j, it), start=(it == 0 and m == 0 and t % 2 == 0),
                                       stop=(it == IT - 1 and m == 2), skip_group_check=True)
                mm.then_inc(s_down, 1)

            turn_xn(0)
            pe.wait_ge(s_xhi, HK)
            pe.wait_ge(s_xlo, HK)
            gate_up(0, 0, True)
            turn_y(1)
            gate_up(0, 1, True)

            def expert_pair(i, first, last):
                for v in range(UB):
                    if v + 2 < UB or not last:
                        gate_up(i, v + 2, first)
                    down(i, v, first)
                    if first and v == 0:
                        turn_xn(1)
                    if first and v == 1:
                        logits()
                    if first and v == 2:
                        turn_logits()
                    if first and v == 3:
                        pe.wait_ge(s_rtv, 2)

            over_expert_pairs(pe, expert_pair)

        @block.vector
        def _(dve):
            dve.wait_ge(s_vec, 16)
            dve.tensor_scalar(half_conv_bias[:], conv_bias, 0.5, None, ALU.mult).then_inc(s_const_v, 1)
            dve.wait_ge(s_inw, 32)
            for et in range(ET):
                cols = slice(et * P, (et + 1) * P)
                dve.tensor_tensor(tapw[:, :, cols], convw[:, :, cols], inw[:, cols].unsqueeze(1).to_broadcast((P, TAPS, P)),
                                  ALU.mult).then_inc(s_tap, 1)

            def inverse_root(r, m, inv, steps, at, turn, between=None):
                dve.wait_ge(steps, at)
                dve.tensor_scalar(m[:, :, 1], m[:, :, 1], EPS, None, ALU.add).then_inc(steps, 1)
                dve.wait_ge(steps, at + 1)
                dve.reciprocal(inv, m[:, :, 1]).then_inc(steps, 1)
                if between:
                    between()
                dve.wait_ge(s_root, turn)
                dve.tensor_tensor(inv, r, r, ALU.mult).then_inc(steps, 1)
                dve.wait_ge(steps, at + 3)
                dve.tensor_tensor(inv, inv, m[:, :, 1], ALU.mult).then_inc(steps, 1)
                dve.wait_ge(steps, at + 4)
                dve.tensor_scalar(inv, inv, -0.5, 1.5, ALU.mult, ALU.add).then_inc(steps, 1)
                dve.wait_ge(steps, at + 5)
                dve.tensor_tensor(r, r, inv, ALU.mult).then_inc(steps, 1)
                dve.wait_ge(steps, at + RS)

            def make_u(n):
                dve.wait_ge(s_half, n + 1)
                dve.scalar_tensor_tensor(u[:, n], tanh_t[:, n], 1.0, half_t[:, n], ALU.add, ALU.mult).then_inc(s_u, 1)

            dve.wait_ge(s_x, 16 * TG)
            for t in range(NT):
                dve.bn_stats(stats[:, t], xs[:, t]).then_inc(s_ln1, 1)
            for t in range(NT):
                dve.wait_ge(s_ln1, t + 1)
                dve.bn_aggr(mv[:, t], stats[:, t]).then_inc(s_ln1, 1)
            make_u(0)
            inverse_root(rstd[:], mv, inv_var[:], s_ln1, 2 * NT, 1, lambda: make_u(1))
            dve.tensor_scalar(half_rstd[:], rstd[:], 0.5, None, ALU.mult).then_inc(s_ln1, 1)
            dve.wait_ge(s_ln1, 2 * NT + RS + 1)
            dve.scalar_tensor_tensor(neg_half_mr[:], mv[:, :, 0], -1.0, half_rstd[:], ALU.mult, ALU.mult).then_inc(s_ln1, 1)
            dve.wait_ge(s_const, 4)
            for et in range(ET):
                dve.tensor_scalar(diag_d[:, et], ident[:], dskip[:, et:et + 1], None, ALU.mult).then_inc(s_const_v, 1)
            make_u(2)
            dve.wait_ge(s_alog, 1)
            dve.tensor_scalar(neg_a[:], exp_alog[:], -1.0, None, ALU.mult).then_inc(s_const_v, 1)

            def bc_left(p):
                dve.wait_ge(s_bca, p + 1)
                if p:
                    dve.wait_ge(s_bcv, 5 * p)
                dve.tensor_tensor(bc_rest[0:DT0, p], ps[0:DT0, x_proj_bank[p]], bc_round[0:DT0], ALU.subtract).then_inc(s_bcv, 1)

            def bc_parts(p):
                dve.tensor_copy(bc[0:BCR, p], bc_round[0:BCR]).then_inc(s_bcv, 1)
                dve.wait_ge(s_bcv, 5 * p + 1)
                dve.tensor_copy(bc_mid[2 * BCR:DT0], bc_rest[2 * BCR:DT0, p]).then_inc(s_bcv, 1)
                dve.tensor_copy(bc[BCR:2 * BCR, p], bc_rest[BCR:2 * BCR, p]).then_inc(s_bcv, 1)
                dve.wait_ge(s_bcv, 5 * p + 3)
                dve.tensor_tensor(bc[2 * BCR:DT0, p], bc_rest[2 * BCR:DT0, p], bc_mid[2 * BCR:DT0], ALU.subtract).then_inc(s_bcv, 1)

            def delta_first(p):
                for et in range(ET):
                    n = p * ET + et
                    at = 4 * ET * p + 3 * et
                    dve.wait_ge(s_spa, 8 * p + 2 * ET + et + 1)
                    dve.tensor_scalar(du[:, n], sp_exp[p][:, et], 1.0, -1.0, ALU.add, ALU.add).then_inc(s_spv, 1)
                    dve.wait_ge(s_spv, at + 1)
                    dve.tensor_tensor(du[:, n], sp_exp[p][:, et], du[:, n], ALU.subtract).then_inc(s_spv, 1)
                    dve.wait_ge(s_spv, at + 2)
                    dve.tensor_tensor(du[:, n], sp_max[p][:, et], du[:, n], ALU.add).then_inc(s_spv, 1)

            def delta_last(p):
                for et in range(ET):
                    n = p * ET + et
                    at = 4 * ET * p + 3 * ET + et
                    dve.wait_ge(s_spv, at)
                    dve.wait_ge(s_spa, 8 * p + 3 * ET + et + 1)
                    flat = delta[:, n].rearrange("p b l -> p (b l)")
                    dve.tensor_tensor(flat, du[:, n], sp_ln[p][:, et], ALU.add).then_inc(s_spv, 1)
                    dve.wait_ge(s_spv, at + 1)
                    dve.tensor_tensor(du[:, n], flat, u[:, n], ALU.mult).then_inc(s_du, 1)

            def gated_z(p):
                for t in range(p * TT, (p + 1) * TT):
                    dve.wait_ge(s_zs, t + 1)
                    dve.scalar_tensor_tensor(zt[:, t], xs[:, t], mv[:, t, 0:1], zt[:, t], ALU.subtract, ALU.mult).then_inc(s_gz, 1)

            bc_left(0)
            bc_parts(0)
            delta_first(0)
            delta_last(0)
            make_u(3)

            gz = zt[:].rearrange("p (q b k) l -> p q b k l", q=PAIRS, b=2)

            def gate_y(p):
                dve.wait_ge(s_gz, TT * (p + 1))
                for et in range(ET):
                    dve.wait_ge(s_sum, (p + 1) * N2 * ET)
                    dve.scalar_tensor_tensor(yg[:, p * ET + et], ps[:, et].rearrange("p (b l) -> p b l", b=2), 0.5,
                                             gz[:, p, :, et], ALU.mult, ALU.mult).then_inc(s_yg, 1)

            for p in range(PAIRS):
                dve.wait_ge(s_du, ET * (p + 1))
                def scans(i):
                    for par in range(2):
                        n2 = 2 * i + (p * N2 + par)
                        start = p == 0 and isinstance(i, int) and i == 0 and par == 0
                        dve.wait_ge(s_rows, n2 + 1)
                        for et in range(ET):
                            if not start:
                                dve.wait_ge(s_state, ET * n2 + et - (ET - 1))
                            dve.tensor_tensor(drive[:, et], du[:, p * ET + et].unsqueeze(1).to_broadcast((P, 2, T)),
                                              ps[:, 2 + 2 * par:4 + 2 * par], ALU.mult).then_inc(s_drive, 1)
                        if start:
                            bc_left(1)
                        for et in range(ET):
                            n = ET * n2 + et
                            dve.wait_ge(s_drive, n + 1)
                            dve.wait_ge(s_decay, 2 * n + 2)
                            if not start:
                                dve.wait_ge(s_prod, n - (ET - 1))
                            dve.tensor_tensor_scan(state[:, et].rearrange("p j t -> p (j t)"),
                                                   decay[:, et].rearrange("p j b l -> p (j b l)"),
                                                   drive[:, et].rearrange("p j t -> p (j t)"),
                                                   0.0, ALU.mult, ALU.add).then_inc(s_state, 1)
                        if p and isinstance(i, int) and i == 0 and par == 0:
                            gate_y(p - 1)
                        first_of_all = p == 0 and isinstance(i, int) and i == 0
                        if first_of_all and par == 0:
                            bc_parts(1)
                        if first_of_all and par == 1:
                            delta_first(1)
                        if p == 0 and isinstance(i, int) and i == N2 // 2 - 1:
                            if par == 0:
                                delta_last(1)
                            else:
                                gated_z(0)
                over_state_pairs(dve, p, scans)
            def second_norm(g, between=None):
                tiles = slice(g * TT, (g + 1) * TT)
                at = (2 * TT + RS) * g
                dve.wait_ge(s_gz, TT * (g + 1))
                dve.wait_ge(s_zt, TT * (g + 1))
                for b in range(2):
                    first_tile = g * TT + 2 * b
                    dve.wait_ge(s_yt, 2 * g + b + 1)
                    x1 = xs[:, first_tile:first_tile + 2].rearrange("p t h -> p (t h)")
                    dve.tensor_tensor(x1, x1, ps[:, (2, 6)[g] + b], ALU.add).then_inc(s_x1, 1)
                for t in range(TT):
                    dve.wait_ge(s_x1, 2 * g + t // 2 + 1)
                    dve.bn_stats(stats2[:, g * TT + t], xs[:, g * TT + t]).then_inc(s_ln2, 1)
                for t in range(TT):
                    dve.wait_ge(s_ln2, at + t + 1)
                    dve.bn_aggr(mv2[:, g * TT + t], stats2[:, g * TT + t]).then_inc(s_ln2, 1)
                inverse_root(rstd2[:, tiles], mv2[:, tiles], inv_var2[:, tiles], s_ln2, at + 2 * TT, 2 + g, between)
                dve.wait_ge(s_state, PAIRS * N2 * ET)
                for t in range(g * TT, (g + 1) * TT):
                    dve.tensor_scalar(xn[:, t], xs[:, t], mv2[:, t, 0:1], rstd2[:, t:t + 1], ALU.subtract,
                                      ALU.mult).then_inc(s_xn, 1)

            def columns_low(g):
                for k in range(HK):
                    dve.wait_ge(s_xhi, HK * g + k + 1)
                    cols = slice(g * T, (g + 1) * T)
                    dve.tensor_tensor(xt_lo[:, k, cols], ps[:, 4 + HK * g + k], xt_hi[:, k, cols].bitcast(F32),
                                      ALU.subtract).then_inc(s_xlo, 1)

            def router():
                over_e = lambda a: a.unsqueeze(2).to_broadcast((P, NT, E))
                capped = ps[:, 6, 0:NT * E].rearrange("p (t e) -> p t e", e=E)
                steps = [0]

                def step(instruction):
                    steps[0] += 1
                    instruction.then_inc(s_rtv, 1)
                    dve.wait_ge(s_rtv, steps[0])

                dve.wait_ge(s_lgt, 1)
                step(dve.tensor_reduce(lg_max[:], capped, AX_X, ALU.max))
                step(dve.tensor_tensor(lg_exp[:], capped, over_e(lg_max[:]), ALU.subtract))
                dve.wait_ge(s_rta, TG + 1)
                step(dve.tensor_reduce(lg_sum[:], lg_exp[:], AX_X, ALU.add))
                step(dve.reciprocal(lg_sum[:], lg_sum[:]))
                dve.wait_ge(s_pad, 6)
                step(dve.tensor_tensor(probs[:, :, 0:E], lg_exp[:], over_e(lg_sum[:]), ALU.mult))
                for t in range(NT):
                    dve.max(top8[:, t], probs[:, t, 0:E]).then_inc(s_rtv, 1)
                steps[0] += NT
                dve.wait_ge(s_rtv, steps[0])
                step(dve.tensor_copy(chosen[:, :, 0:TOPK], top8[:, :, 0:TOPK]))
                for t in range(NT):
                    dve.match_replace(others[:, t], chosen[:, t], probs[:, t], 0.0).then_inc(s_rtv, 1)
                steps[0] += NT
                dve.wait_ge(s_rtv, steps[0])
                step(dve.tensor_tensor(weight[:], probs[:, :, 0:E], others[:, :, 0:E], ALU.subtract))

            second_norm(0)
            dve.wait_ge(s_small, 48)
            dve.wait_ge(s_wgz, 2)
            dve.tensor_copy(wg_hi[:, :, 0:E], wg[:]).then_inc(s_wg, 1)
            dve.wait_ge(s_wg, 1)
            dve.tensor_tensor(wg_lo[:, :, 0:E], wg[:], wg_hi[:, :, 0:E].bitcast(F32), ALU.subtract).then_inc(s_wg, 1)
            columns_low(0)
            gated_z(1)
            gate_y(PAIRS - 1)

            weight_q = weight[:].rearrange("p t (i j) -> p t i j", j=2)

            def add_expert(i, j, g):
                dve.wait_ge(s_down, UB * i + (j * UE + (g + 1) * IT))
                for t in range(TT):
                    a = g * TT + t
                    dve.scalar_tensor_tensor(xs[:, a], ps[:, 4 + 2 * g + t // 2, t % 2 * H:(t % 2 + 1) * H],
                                             weight_q[:, a, i, j:j + 1], xs[:, a], ALU.mult, ALU.add).then_inc(s_acc, 1)

            def hidden(i, v, first):
                n = UB * i + v
                dve.wait_ge(s_gt, n + 1)
                if not first or v >= 2:
                    dve.wait_ge(s_hid, n - 1)
                dve.scalar_tensor_tensor(g_silu2[:, v % 2], g_tanh[:, v % 2], 1.0, ps[:, gate_bank(v)], ALU.add,
                                         ALU.mult).then_inc(s_gs, 1)
                dve.wait_ge(s_gs, n + 1)
                dve.wait_ge(s_up, n + 1)
                if not first or v >= 2:
                    dve.wait_ge(s_hlo, n - 1)
                dve.scalar_tensor_tensor(hid[:, v % 2], g_silu2[:, v % 2], 0.5, ps[:, gate_bank(v) + 1], ALU.mult,
                                         ALU.mult).then_inc(s_hid, 1)

            def expert_pair(i, first, last):
                for v in range(UB):
                    if first and v == 1:
                        continue
                    hidden(i, v, first)
                    if first and v == 0:
                        second_norm(1, lambda: hidden(i, 1, first))
                    if first and v == 2:
                        columns_low(1)
                    if first and v == 3:
                        router()
                    if v == 2 and not first:
                        add_expert(i - 1, 1, TG - 1)
                    if v in (6, 10, 14):
                        add_expert(i, (v - 3) // UE, (v - 3) // IT % TG)

            over_expert_pairs(dve, expert_pair)
            add_expert(E // 2 - 1, 1, TG - 1)


def kernel(x, ctx_1024, L0_xattn_in_proj_w, L0_xattn_conv_w, L0_xattn_conv_b, L0_xattn_x_proj_w, L0_xattn_dt_proj_w,
           L0_xattn_dt_proj_b, L0_xattn_A_log, L0_xattn_D, L0_ffn_w_gate, L0_ffn_w1, L0_ffn_w3, L0_ffn_w2):
    import numpy as np
    import concourse.bacc as bacc
    from concourse.bass_utils import run_bass_kernel_spmd

    x_proj_t = np.transpose(L0_xattn_x_proj_w)
    dt_rank = L0_xattn_dt_proj_w.shape[1]
    given = {
        "x": x, "ctx_t": np.transpose(ctx_1024, (2, 0, 1)), "in_proj_t": np.transpose(L0_xattn_in_proj_w),
        "conv_w_t": np.transpose(L0_xattn_conv_w),
        "channel_rows": np.concatenate([L0_xattn_conv_b[:, None], L0_xattn_dt_proj_b[:, None],
                                        L0_xattn_D[:, None], L0_xattn_A_log], axis=1),
        "x_proj_rows": np.concatenate([x_proj_t[:, dt_rank:]] * 3 + [x_proj_t[:, :dt_rank]], axis=1),
        "dt_proj_t": np.transpose(L0_xattn_dt_proj_w),
        "w_gate": L0_ffn_w_gate, "w1": L0_ffn_w1, "w3": L0_ffn_w3, "w2": L0_ffn_w2,
    }
    nc = bacc.Bacc("TRN2", target_bir_lowering=False, num_devices=1)
    arrays, args = {}, {}
    for name, a in given.items():
        a = np.ascontiguousarray(a)
        arrays[f"in_{name}"] = a
        args[name] = nc.dram_tensor(f"in_{name}", a.shape, mybir.dt.from_np(a.dtype), kind="ExternalInput").ap()
    out = nc.dram_tensor("out", x.shape, F32, kind="ExternalOutput").ap()
    xattn_ffn(nc, **args, out=out)
    r = run_bass_kernel_spmd(nc, [arrays], core_ids=[0])
    return r.results[0]["out"]
```

```python
from contextlib import ExitStack

import concourse.bass as bass
from concourse import mybir

P = 128
ALU = mybir.AluOpType
ACT = mybir.ActivationFunctionType
F32 = mybir.dt.float32
F32R = mybir.dt.float32r
BF16 = mybir.dt.bfloat16
AX_X = mybir.AxisListType.X

EPS = 1e-5
SOFTCAP = 30.0
TOPK = 2
WARM_UP = 13
RS = 6


def xattn_ffn(nc, x, ctx_t, in_proj_t, conv_w_t, channel_rows, x_proj_rows, dt_proj_t, w_gate, w1, w3, w2, out):
    DM, B, L = ctx_t.shape
    DI = in_proj_t.shape[1]
    TAPS = conv_w_t.shape[0]
    DR = dt_proj_t.shape[0]
    DS = channel_rows.shape[1] - 3
    E, H, I = w1.shape
    assert DM == P and DI == L == H == 2 * P and DS == 16
    PAD = TAPS - 1
    ET = DI // P
    PAIRS = B // 2
    T = 2 * L
    NT = B * L // P
    N2 = DS // 2
    BCR = 2 * DS
    DT0 = 3 * BCR
    HK = H // P
    IT = I // P
    TG = B * L // T
    TT = T // P
    UE = TG * IT
    UB = 2 * UE
    WCOLS = 2 * HK * I + IT * H
    W3_AT, W2_AT = HK * I, 2 * HK * I

    with ExitStack() as ctx:
        def sb(name, shape, dt=F32):
            return ctx.enter_context(nc.sbuf_tensor(name, shape, dt))

        def sem(name):
            return ctx.enter_context(nc.semaphore(name))

        ctx_pad = sb("ctx_pad", [P, B, L + PAD])
        inw = sb("inw", [P, DI])
        tapw = sb("tapw", [P, TAPS, DI])
        channel = sb("channel", [P, ET, 3 + DS])
        conv_bias, dt_bias, dskip, alog = channel[:, :, 0], channel[:, :, 1], channel[:, :, 2], channel[:, :, 3:]
        half_conv_bias = sb("half_conv_bias", [P, ET])
        xpw = sb("xpw", [P, ET, DT0 + DR])
        dtw = sb("dtw", [P, DI])
        exp_alog = sb("exp_alog", [P, ET, DS])
        neg_a = sb("neg_a", [P, ET, DS])
        diag_d = sb("diag_d", [P, ET, P])
        ident = sb("ident", [P, P])
        ident_bc = sb("ident_bc", [P, BCR], BF16)
        select = sb("select", [P, BCR, P], BF16)
        xs = sb("xs", [P, NT, H])
        wg = sb("wg", [P, HK, E])
        wg_parts = sb("wg_parts", [P, HK, P], F32R)

        warm = bc_mid = sb("bc_mid", [P, T], BF16)

        tanh_t = sb("tanh_t", [P, PAIRS * ET, T])
        u = sb("u", [P, PAIRS * ET, T])
        convw = u[:, 0:2].rearrange("p n (k e) -> p (n k) e", e=DI)
        bc_round = sb("bc_round", [P, T], BF16)
        bc = sb("bc", [P, PAIRS, T], BF16)
        dt_lo = sb("dt_lo", [P, PAIRS, T])
        delta = sb("delta", [P, PAIRS * ET, 2, L])
        du = sb("du", [P, PAIRS * ET, T])

        stats = sb("stats", [P, NT, 6])
        mv = sb("mv", [P, NT, 2])
        rstd = sb("rstd", [P, NT])
        inv_var = sb("inv_var", [P, NT])
        half_rstd = sb("half_rstd", [P, NT])
        neg_half_mr = sb("neg_half_mr", [P, NT])
        zt = sb("zt", [P, NT, L])

        decay = sb("decay", [P, ET, 2, 2, L])
        drive = sb("drive", [P, ET, 2, T])
        state = sb("state", [P, ET, 2, T])
        states = ((state[:, 0], state[:, 1]),
                  (tapw[:].rearrange("p k e -> p (k e)")[:, 0:2 * T].rearrange("p (j t) -> p j t", j=2),
                   ctx_pad[:].rearrange("p b l -> p (b l)")[:, 0:2 * T].rearrange("p (j t) -> p j t", j=2)))
        c_rows = sb("c_rows", [P, 2, 2, T])
        prod = sb("prod", [P, ET, 2, T])
        w_raw = sb("w_raw", [P, WCOLS])
        scratch = w_raw[:].rearrange("p (n t) -> p n t", t=T)
        sp_exp = (state[:, 0], scratch[:, 0:2])
        sp_ln = (state[:, 1], scratch[:, 2:4])
        sp_max = (drive[:, 0], scratch[:, 4:6])
        half_t = prod[:].rearrange("p a b t -> p (a b) t")
        bc_rest = c_rows[:, :, 1]
        yg = tanh_t[:].rearrange("p n (b l) -> p n b l", b=2)

        ps = ctx.enter_context(nc.psum_tensor("ps", [P, 8, T], F32))

        stats2 = sb("stats2", [P, NT, 6])
        mv2 = sb("mv2", [P, NT, 2])
        rstd2 = sb("rstd2", [P, NT])
        inv_var2 = sb("inv_var2", [P, NT])
        xn = decay[:].rearrange("p a b c h -> p (a b c) h")
        xt_hi = sb("xt_hi", [P, HK, B * L], F32R)
        xt_lo = sb("xt_lo", [P, HK, B * L], F32R)
        lg_cols = u[:, 0:TG]
        lg_tanh = sb("lg_tanh", [P, NT, E])
        lg_turned = ps[:, 6].rearrange("p (t c) -> p t c", t=NT)
        lg_max = sb("lg_max", [P, NT])
        lg_exp = sb("lg_exp", [P, NT, E])
        lg_sum = sb("lg_sum", [P, NT])
        probs = sb("probs", [P, NT, E + 8 - TOPK])
        top8 = sb("top8", [P, NT, 8])
        chosen = sb("chosen", [P, NT, 8])
        others = sb("others", [P, NT, E + 8 - TOPK])
        weight = sb("weight", [P, NT, E])

        w_hi = sb("w_hi", [P, 2, WCOLS], F32R)
        w_lo = sb("w_lo", [P, 2, WCOLS], F32R)
        g_tanh, g_silu2 = state[:, 0], state[:, 1]
        hid = drive[:, 0]
        hid_hi = sb("hid_hi", [P, 2, T], F32R)
        hid_lo = sb("hid_lo", [P, 2, T], F32R)

        def gate_bank(v):
            return 2 - 2 * (v % 2)

        s_small = sem("small_landed")
        s_vec = sem("vectors_landed")
        s_ctx = sem("ctx_of_pair_0_landed")
        s_ctx1 = sem("ctx_of_pair_1_landed")
        s_x = sem("x_landed")
        s_raw = sem("raw_landed")
        s_inw = sem("in_proj_landed")
        s_out = sem("out_stored")
        s_const = sem("constants_built")
        s_warm = sem("warm_up_zeros")
        s_pad = sem("pads_cleared")
        s_tap = sem("tap_weights_ready")
        s_const_v = sem("vector_constants_ready")
        s_alog = sem("exp_alog_ready")
        s_conv = sem("conv_done")
        s_tanh = sem("conv_tanh_done")
        s_half = sem("conv_half_done")
        s_selm = sem("select_ready")
        s_u = sem("u_done")
        s_xp = sem("x_proj_done")
        s_bca = sem("bc_rounded")
        s_bcv = sem("bc_parts_vector")
        s_dtlo = sem("dt_lo_ready")
        s_dt = sem("dt_proj_done")
        s_spa = sem("softplus_scalar_steps")
        s_spv = sem("softplus_vector_steps")
        s_spp = sem("softplus_gpsimd_steps")
        s_du = sem("du_ready")
        s_ln1 = sem("ln1_steps")
        s_root = sem("variance_root_done")
        s_zt = sem("z_tanh_done")
        s_zs = sem("z_tanh_scaled")
        s_gz = sem("gated_z_ready")
        s_rows = sem("bc_rows_broadcast")
        s_crow = sem("c_rows_copied")
        s_decay = sem("decay_ready")
        s_drive = sem("drive_ready")
        s_state = sem("state_ready")
        s_prod = sem("prod_ready")
        s_sum = sem("prod_summed")
        s_yg = sem("yg_ready")
        s_yt = sem("y_turned")
        s_x1 = sem("x1_ready")
        s_ln2 = sem("ln2_steps")
        s_xn = sem("xn_ready")
        s_xt = sem("xn_turned")
        s_xhi = sem("xt_hi_ready")
        s_xlo = sem("xt_lo_ready")
        s_wgz = sem("gate_weight_pads_cleared")
        s_lgc = sem("logit_columns_copied")
        s_lgl = sem("logit_low_share_copied")
        s_lga = sem("logit_shares_added")
        s_lgt = sem("logits_in_token_rows")
        s_lg = sem("logits_done")
        s_rta = sem("router_scalar_steps")
        s_rtv = sem("router_vector_steps")
        s_whi = sem("w_hi_ready")
        s_wlo = sem("w_lo_ready")
        s_wg = sem("gate_weights_split")
        s_gate = sem("gate_done")
        s_up = sem("up_done")
        s_gt = sem("gate_tanh_done")
        s_gs = sem("gate_silu_done")
        s_hid = sem("hid_done")
        s_hhi = sem("hid_hi_done")
        s_hlo = sem("hid_lo_done")
        s_down = sem("down_unit_done")
        s_half_down = sem("last_down_first_bank_done")
        s_acc = sem("down_added")

        x_proj_bank, dt_bank = (6, 5), (0, 4)

        x_rows = x.rearrange("b (t p) h -> p (b t) h", p=P)
        out_rows = out.rearrange("b (t p) h -> p (b t) h", p=P)
        w1_d = w1.rearrange("e (k p) i -> e p k i", p=P)
        w3_d = w3.rearrange("e (k p) i -> e p k i", p=P)
        w2_d = w2.rearrange("e (k p) h -> e p k h", p=P)

        block = ctx.enter_context(nc.Block())

        stores = ((0, TT), (TT, NT - 2), (NT - 2, NT - 1), (NT - 1, NT))

        @block.sync
        def _(sp):
            sp.dma_start(inw[:], in_proj_t).then_inc(s_inw, 16)
            sp.dma_start(convw, conv_w_t.rearrange("(o k) e -> o k e", o=1).to_broadcast((P, TAPS, DI))).then_inc(s_inw, 16)
            sp.dma_start(ctx_pad[:, 2:4, PAD:], ctx_t[:, 2:4]).then_inc(s_ctx1, 16)
            sp.dma_start(xpw[:], x_proj_rows.rearrange("(k p) c -> p k c", p=P)).then_inc(s_small, 16)
            sp.dma_start(dtw[DT0:DT0 + DR, :], dt_proj_t).then_inc(s_small, 16)
            sp.dma_start(wg[:], w_gate.rearrange("(k p) e -> p k e", p=P)).then_inc(s_small, 16)

            def load_expert(e):
                for at, w, k in ((0, w1_d, HK), (W3_AT, w3_d, HK), (W2_AT, w2_d, IT)):
                    sp.dma_start(w_raw[:, at:at + WCOLS // 3].rearrange("p (k i) -> p k i", k=k),
                                 w[e].rearrange("o p k i -> (o p) k i")).then_inc(s_raw, 16)

            sp.wait_ge(s_du, PAIRS * ET)
            load_expert(slice(0, 1))
            with sp.Fori(0, E - 1) as e:
                sp.wait_ge(s_whi, IT * e + IT)
                sp.wait_ge(s_wlo, IT * e + IT)
                load_expert(bass.ds(e + 1, 1))
            for a, b in stores:
                sp.wait_ge(s_acc, (E - 1) * NT + b)
                sp.dma_start(out_rows[:, a:b], xs[:, a:b]).then_inc(s_out, 16)
            sp.wait_ge(s_out, 16 * len(stores))

        def over_state_pairs(engine, p, body):
            body(0)
            with engine.Fori(1, N2 // 2 - 1) as i:
                body(i)
            body(N2 // 2 - 1)

        def over_expert_pairs(engine, body):
            body(0, True, False)
            with engine.Fori(1, E // 2 - 1) as i:
                body(i, False, False)
            body(E // 2 - 1, False, True)

        @block.gpsimd
        def _(pool):
            pool.memset(warm[:], 0.0).then_inc(s_warm, 1)
            pool.memset(ctx_pad[:, :, 0:PAD], 0.0).then_inc(s_pad, 1)
            pool.memset(ident_bc[:], 0.0).then_inc(s_pad, 1)
            pool.memset(ident[:], 0.0).then_inc(s_pad, 1)
            pool.wait_ge(s_pad, 2)
            for copy in range(3):
                pool.affine_select(out=ident_bc[:], in_=ident_bc[:], compare_op=ALU.not_equal, fill=1.0,
                                   base=-copy * BCR, pattern=[[-1, BCR]], channel_multiplier=1).then_inc(s_const, 1)
                pool.wait_ge(s_const, copy + 1)
            pool.wait_ge(s_pad, 3)
            pool.affine_select(out=ident[:], in_=ident[:], compare_op=ALU.not_equal, fill=1.0, base=0,
                               pattern=[[-1, P]], channel_multiplier=1).then_inc(s_const, 1)
            pool.tensor_copy(select[:], ident_bc[:].unsqueeze(2).to_broadcast((P, BCR, P))).then_inc(s_selm, 1)
            pool.memset(decay[:, :, :, :, 0:1].rearrange("p a b c o -> p (a b c) o"), 0.0).then_inc(s_pad, 1)
            pool.memset(probs[:], -1.0).then_inc(s_pad, 1)
            pool.memset(chosen[:], -1.0).then_inc(s_pad, 1)
            pool.memset(wg_parts[:].bitcast(F32), 0.0).then_inc(s_wgz, 1)

            def delta_middle(n):
                pool.wait_ge(s_spv, 4 * ET + 1)
                pool.tensor_tensor(du[:, n], sp_exp[1][:, n - ET], du[:, n], ALU.subtract).then_inc(s_spp, 1)
                pool.wait_ge(s_spp, 1)
                pool.tensor_tensor(du[:, n], sp_max[1][:, n - ET], du[:, n], ALU.add).then_inc(s_spp, 1)

            pool.wait_ge(s_u, PAIRS * ET)
            for p in range(PAIRS):
                def c_products(i):
                    for par in range(2):
                        n2 = 2 * i + (p * N2 + par)
                        for et in range(ET):
                            n = ET * n2 + et
                            pool.wait_ge(s_state, n + 1)
                            pool.wait_ge(s_crow, n2 + 1)
                            if not (p == 0 and isinstance(i, int) and i == 0 and par == 0):
                                pool.wait_ge(s_sum, n - (ET - 1))
                            pool.tensor_tensor(prod[:, et], states[par][et], c_rows[:, par], ALU.mult).then_inc(s_prod, 1)
                        if p == 0 and isinstance(i, int) and i == 0 and par == 0:
                            delta_middle(ET)
                over_state_pairs(pool, p, c_products)

            def split_low(e, j, q):
                n = WCOLS // IT
                pool.wait_ge(s_whi, IT * e + (q + 1))
                pool.tensor_tensor(w_lo[:, j, q * n:(q + 1) * n], w_raw[:, q * n:(q + 1) * n],
                                   w_hi[:, j, q * n:(q + 1) * n].bitcast(F32), ALU.subtract).then_inc(s_wlo, 1)

            for q in range(IT):
                split_low(0, 0, q)

            def expert_pair(i, first, last):
                for v in range(UB):
                    n = UB * i + v
                    pool.wait_ge(s_hhi, n + 1)
                    if not first or v >= 2:
                        pool.wait_ge(s_down, n - 1)
                    pool.tensor_tensor(hid_lo[:, v % 2], hid[:, v % 2], hid_hi[:, v % 2].bitcast(F32),
                                       ALU.subtract).then_inc(s_hlo, 1)
                    if 2 <= v % UE < 2 + IT and (v < UE or not last):
                        split_low(2 * i + (1 + v // UE), 1 - v // UE, v % UE - 2)

            over_expert_pairs(pool, expert_pair)

        @block.scalar
        def _(act):
            act.dma_start(ctx_pad[:, 0:2, PAD:], ctx_t[:, 0:2]).then_inc(s_ctx, 16)
            act.dma_start(channel[:], channel_rows.rearrange("(k p) c -> p k c", p=P)).then_inc(s_vec, 16)
            for g in range(TG):
                act.dma_start(xs[:, g * TT:(g + 1) * TT], x_rows[:, g * TT:(g + 1) * TT]).then_inc(s_x, 16)
            act.wait_ge(s_vec, 16)
            act.activation(exp_alog[:], alog, ACT.Exp).then_inc(s_alog, 1)

            act.wait_ge(s_const_v, 1)

            def conv_halves(n):
                bias = half_conv_bias[:, n % ET:n % ET + 1]
                act.wait_ge(s_conv, n + 1)
                act.activation(tanh_t[:, n], ps[:, 2 + n], ACT.Tanh, scale=0.5, bias=bias).then_inc(s_tanh, 1)
                act.activation(half_t[:, n], ps[:, 2 + n], ACT.Identity, scale=0.5, bias=bias).then_inc(s_half, 1)

            def z_tanh(tiles):
                for t in tiles:
                    act.activation(zt[:, t], xs[:, t], ACT.Tanh, scale=half_rstd[:, t:t + 1],
                                   bias=neg_half_mr[:, t:t + 1]).then_inc(s_zt, 1)

            def z_scale(tiles):
                for t in tiles:
                    act.wait_ge(s_zt, t + 1)
                    act.activation(zt[:, t], zt[:, t], ACT.Identity, scale=rstd[:, t:t + 1], bias=rstd[:, t:t + 1]).then_inc(s_zs, 1)

            def round_bc(p):
                bank = x_proj_bank[p]
                act.wait_ge(s_xp, p + 1)
                act.activation(dt_lo[DT0:DT0 + DR, p], ps[DT0:DT0 + DR, bank], ACT.Copy).then_inc(s_dtlo, 1)
                if p:
                    act.wait_ge(s_bcv, 5 * p)
                act.activation(bc_round[0:DT0], ps[0:DT0, bank], ACT.Copy).then_inc(s_bca, 1)

            def softplus_in(p):
                for et in range(ET):
                    act.wait_ge(s_dt, p * ET + et + 1)
                    act.activation(sp_exp[p][:, et], ps[:, dt_bank[p] + et], ACT.Abs, bias=dt_bias[:, et:et + 1]).then_inc(s_spa, 1)
                    act.activation(sp_max[p][:, et], ps[:, dt_bank[p] + et], ACT.Relu, bias=dt_bias[:, et:et + 1]).then_inc(s_spa, 1)

            def softplus_exp(p):
                for et in range(ET):
                    act.wait_ge(s_spa, 8 * p + 2 * et + 1)
                    act.activation(sp_exp[p][:, et], sp_exp[p][:, et], ACT.Exp, scale=-1.0).then_inc(s_spa, 1)

            def softplus_ln(p):
                for et in range(ET):
                    act.wait_ge(s_spa, 8 * p + 2 * ET + et + 1)
                    act.activation(sp_ln[p][:, et], sp_exp[p][:, et], ACT.Ln, bias=1.0).then_inc(s_spa, 1)

            conv_halves(0)
            conv_halves(1)
            round_bc(0)
            softplus_in(0)
            softplus_exp(0)
            softplus_ln(0)
            act.wait_ge(s_ln1, 2 * NT + 2)
            act.activation(rstd[:], inv_var[:], ACT.Ln).then_inc(s_root, 1)
            conv_halves(2)
            conv_halves(3)
            act.wait_ge(s_root, 1)
            act.activation(rstd[:], rstd[:], ACT.Exp, scale=0.5).then_inc(s_root, 1)

            neg_a_q = neg_a[:].rearrange("p k (i q) -> p k i q", q=4)
            act.wait_ge(s_pad, 4)
            act.wait_ge(s_const_v, 4)

            def split_high(j, q):
                n = WCOLS // IT
                act.activation(w_hi[:, j, q * n:(q + 1) * n], w_raw[:, q * n:(q + 1) * n], ACT.Copy).then_inc(s_whi, 1)

            for p in range(PAIRS):
                def decays(i):
                    for par in range(2):
                        n2 = 2 * i + (p * N2 + par)
                        start = p == 0 and isinstance(i, int) and i == 0
                        act.wait_ge(s_rows, n2 + 1)
                        if start and par:
                            act.wait_ge(s_bcv, 5 * PAIRS)
                        if not start:
                            act.wait_ge(s_prod, ET * n2 - ET)
                        act.activation(c_rows[:, par], ps[:, 6:8], ACT.Copy).then_inc(s_crow, 1)
                        for et in range(ET):
                            if not (start and par == 0):
                                act.wait_ge(s_state, ET * n2 + et - (ET - 1))
                            if isinstance(i, int) and i == 0 and par == 0:
                                act.wait_ge(s_spv, 3 * ET * (p + 1) + et + 1)
                            for j in range(2):
                                act.activation(decay[:, et, j, :, 1:], delta[:, p * ET + et, :, 1:], ACT.Exp,
                                               scale=neg_a_q[:, et, i, 2 * par + j:2 * par + j + 1]).then_inc(s_decay, 1)
                        if start and par == 0:
                            round_bc(1)
                            softplus_in(1)
                            softplus_exp(1)
                        if start and par == 1:
                            softplus_ln(1)
                        if p == 0 and isinstance(i, int) and i == N2 // 2 - 1:
                            if par == 0:
                                act.wait_ge(s_ln1, 2 * NT + RS + 2)
                                z_tanh(range(0, TT))
                            else:
                                z_scale(range(0, TT))
                        if p == PAIRS - 1 and isinstance(i, int) and i == N2 // 2 - 1:
                            if par == 0:
                                act.wait_ge(s_raw, 48)
                            split_high(0, 2 * par)
                            split_high(0, 2 * par + 1)
                over_state_pairs(act, p, decays)

            def second_root(g):
                act.wait_ge(s_ln2, (2 * TT + RS) * g + 2 * TT + 2)
                act.activation(rstd2[:, g * TT:(g + 1) * TT], inv_var2[:, g * TT:(g + 1) * TT], ACT.Sqrt).then_inc(s_root, 1)

            def columns_high(g):
                for k in range(HK):
                    act.wait_ge(s_xt, HK * g + k + 1)
                    act.activation(xt_hi[:, k, g * T:(g + 1) * T], ps[:, 4 + HK * g + k], ACT.Copy).then_inc(s_xhi, 1)

            z_tanh(range(NT // 2, NT))
            second_root(0)
            z_scale(range(NT // 2, NT))
            columns_high(0)

            def expert_pair(i, first, last):
                for v in range(UB):
                    n = UB * i + v
                    act.wait_ge(s_gate, n + 1)
                    if not first or v >= 2:
                        act.wait_ge(s_gs, n - 1)
                    act.activation(g_tanh[:, v % 2], ps[:, gate_bank(v)], ACT.Tanh, scale=0.5).then_inc(s_gt, 1)
                    if first and v == 1:
                        second_root(1)
                    if first and v == 2:
                        columns_high(1)
                    if first and v == 3:
                        for g in range(TG):
                            act.wait_ge(s_lg, g + 1)
                            act.activation(lg_cols[0:2 * BCR, g], ps[0:2 * BCR, 6 + g], ACT.Copy).then_inc(s_lgc, 1)
                    if 2 <= v % UE < 2 + IT and (v < UE or not last):
                        if v % UE == 2:
                            act.wait_ge(s_raw, 96 * i + (96 + 48 * (v // UE)))
                            if not first or v >= UE:
                                act.wait_ge(s_down, UB * i + v // UE * UE)
                        split_high(1 - v // UE, v % UE - 2)
                    act.wait_ge(s_hid, n + 1)
                    if not first or v >= 2:
                        act.wait_ge(s_down, n - 1)
                    act.activation(hid_hi[:, v % 2], hid[:, v % 2], ACT.Copy).then_inc(s_hhi, 1)
                    if first and v == 3:
                        act.wait_ge(s_lgt, 1)
                        act.activation(lg_tanh[:], lg_turned[:, :, BCR:BCR + E], ACT.Copy).then_inc(s_lgl, 1)
                        act.wait_ge(s_lga, 1)
                        act.activation(lg_tanh[:], lg_tanh[:], ACT.Tanh, scale=1.0 / SOFTCAP).then_inc(s_rta, 1)
                        act.wait_ge(s_rtv, 2)
                        act.activation(lg_exp[:], lg_exp[:], ACT.Exp, scale=SOFTCAP).then_inc(s_rta, 1)

            over_expert_pairs(act, expert_pair)

        @block.tensor
        def _(pe):
            pe.wait_ge(s_warm, 1)
            for n in range(WARM_UP):
                pe.matmul(ps[:, 0], warm[:, 0:P], warm[:], start=True, stop=True)
            pe.wait_ge(s_tap, 1)
            pe.wait_ge(s_pad, 1)
            pe.wait_ge(s_ctx, 16)

            def convolution(n, taps=range(TAPS)):
                p, et = n // ET, n % ET
                for k in taps:
                    mm = pe.matmul(ps[:, 2 + n].rearrange("p (b l) -> p b l", b=2), tapw[:, k, et * P:(et + 1) * P],
                                   ctx_pad[:, 2 * p:2 * p + 2, k:k + L], start=(k == 0), stop=(k == TAPS - 1))
                if taps[-1] == TAPS - 1:
                    mm.then_inc(s_conv, 1)

            def x_proj(p):
                if p:
                    pe.wait_ge(s_half, PAIRS * ET)
                for k in range(ET):
                    pe.wait_ge(s_u, p * ET + k + 1)
                    mm = pe.matmul(ps[0:DT0 + DR, x_proj_bank[p]], xpw[:, k, :], u[:, p * ET + k], start=(k == 0),
                                   stop=(k == ET - 1))
                mm.then_inc(s_xp, 1)

            def dt_proj(p):
                pe.wait_ge(s_dtlo, p + 1)
                for et in range(ET):
                    if p and et:
                        pe.wait_ge(s_bcv, 5 * p + 1)
                    pe.matmul(ps[:, dt_bank[p] + et], dtw[DT0:DT0 + DR, et * P:(et + 1) * P], dt_lo[DT0:DT0 + DR, p],
                              start=True, stop=True).then_inc(s_dt, 1)

            convolution(0)
            pe.wait_ge(s_tap, 2)
            convolution(1)
            pe.wait_ge(s_ctx1, 16)
            convolution(2, range(0, 2))
            pe.wait_ge(s_small, 48)
            x_proj(0)
            dt_proj(0)
            convolution(2, range(2, TAPS))
            convolution(3)

            def broadcast_rows(p, i, par):
                for at, bank in ((0, 2 + 2 * par), (DS, 6)):
                    for j in range(2):
                        row = 4 * i + (at + 2 * par + j)
                        sel = select[0:DT0, row, :] if isinstance(row, int) else \
                            select[0:DT0, bass.ds(row, 1), :].rearrange("p o m -> p (o m)")
                        mm = pe.matmul(ps[:, bank + j], sel, bc[0:DT0, p], start=True, stop=True)
                mm.then_inc(s_rows, 1)

            pe.wait_ge(s_selm, 1)
            pe.wait_ge(s_bcv, 5)
            broadcast_rows(0, 0, 0)
            pe.wait_ge(s_const_v, 3)
            pe.wait_ge(s_spa, 2 * ET)
            def add_skip(p, opens):
                for et in range(ET):
                    pe.matmul(ps[:, et], diag_d[:, et], u[:, p * ET + et], start=opens, stop=False, skip_group_check=True)

            def turn_y(p):
                pe.wait_ge(s_yg, ET * (p + 1))
                for t in range(TT):
                    b, half = t // 2, t % 2
                    for et in range(ET):
                        mm = pe.transpose(ps[:, (2, 6)[p] + b, half * DI + et * P:half * DI + (et + 1) * P],
                                          yg[:, p * ET + et, b, half * P:(half + 1) * P], ident[:])
                    if half:
                        mm.then_inc(s_yt, 1)

            for p in range(PAIRS):
                if p == 0:
                    add_skip(p, True)
                    x_proj(1)
                    dt_proj(1)
                    pe.wait_ge(s_spa, 6 * ET)
                    pe.wait_ge(s_bcv, 5 + 1)
                    pe.wait_ge(s_crow, 1)
                    broadcast_rows(0, 0, 1)

                def sum_products(i, par, n2):
                    opens = p > 0 and isinstance(i, int) and i == 0 and par == 0
                    final = isinstance(i, int) and i == N2 // 2 - 1 and par == 1
                    if opens:
                        pe.wait_ge(s_yg, ET * p)
                    for et in range(ET):
                        pe.wait_ge(s_prod, ET * n2 + (et + 1))
                        for j in range(2):
                            mm = pe.matmul(ps[:, et], ident[:], prod[:, et, j], start=opens and j == 0,
                                           stop=final and j == 1, skip_group_check=True)
                        mm.then_inc(s_sum, 1)

                def sums(i):
                    for par in range(2):
                        n2 = 2 * i + (p * N2 + par)
                        last = isinstance(i, int) and i == N2 // 2 - 1
                        start = p == 0 and isinstance(i, int) and i == 0
                        if start:
                            sum_products(i, par, n2)
                        if last and p == PAIRS - 1:
                            if par == 0:
                                pe.wait_ge(s_drive, ET * n2 + ET)
                                turn_y(0)
                            else:
                                add_skip(p, False)
                        else:
                            pe.wait_ge(s_drive, ET * n2 + ET)
                            pe.wait_ge(s_crow, n2 + 2)
                            if last:
                                pe.wait_ge(s_bcv, 5 * (p + 2))
                                broadcast_rows(p + 1, 0, par)
                            else:
                                broadcast_rows(p, i + 1, par)
                        if not start:
                            sum_products(i, par, n2)
                over_state_pairs(pe, p, sums)

            def turn_xn(g):
                pe.wait_ge(s_xn, TT * (g + 1))
                for k in range(HK):
                    for t in range(TT):
                        mm = pe.transpose(ps[:, 4 + HK * g + k, t * P:(t + 1) * P], xn[:, g * TT + t, k * P:(k + 1) * P], ident[:])
                    mm.then_inc(s_xt, 1)

            def logits():
                pe.wait_ge(s_wg, 2)
                pe.wait_ge(s_xhi, HK * TG)
                pe.wait_ge(s_xlo, HK * TG)
                for g in range(TG):
                    for k in range(HK):
                        for m, xa in enumerate((xt_hi, xt_lo)):
                            mm = pe.matmul(ps[:, 6 + g], wg_parts[:, k, :], xa[:, k, g * T:(g + 1) * T],
                                           start=(k == 0 and m == 0), stop=(k == HK - 1 and m == 1))
                    mm.then_inc(s_lg, 1)

            def turn_logits():
                pe.wait_ge(s_lgc, TG)
                for t in range(NT):
                    mm = pe.transpose(lg_turned[:, t], lg_cols[0:2 * BCR, t // TT, t % TT * P:(t % TT + 1) * P],
                                      ident[0:2 * BCR, 0:2 * BCR])
                mm.then_inc(s_lgt, 1)

            w1_of = lambda w, j, k, it: w[:, j, k * I + it * P:k * I + (it + 1) * P]
            w3_of = lambda w, j, k, it: w[:, j, W3_AT + k * I + it * P:W3_AT + k * I + (it + 1) * P]
            w2_of = lambda w, j, it: w[:, j, W2_AT + it * H:W2_AT + (it + 1) * H]

            def gate_up(i, v, first):
                n = UB * i + v
                j, g, it, par = v // UE % 2, v // IT % TG, v % IT, v % 2
                for made, of, bank, freed, pieces in ((s_gate, w1_of, gate_bank(par), s_gs, 2), (s_up, w3_of, gate_bank(par) + 1, s_hid, 3)):
                    if not (first and v < 2):
                        pe.wait_ge(freed, n - 1)
                    if v % UE == 0:
                        pe.wait_ge(s_wlo, 2 * IT * i + (v // UE * IT + pieces))
                    for k in range(HK):
                        for m, (wa, xa) in enumerate(((w_hi, xt_hi), (w_hi, xt_lo), (w_lo, xt_hi))):
                            mm = pe.matmul(ps[:, bank], of(wa, j, k, it), xa[:, k, g * T:(g + 1) * T],
                                           start=(k == 0 and m == 0), stop=(k == HK - 1 and m == 2))
                    mm.then_inc(made, 1)

            def down(i, v, first, final):
                n = UB * i + v
                j, g, it, par = v // UE, v // IT % TG, v % IT, v % 2
                if v % UE == 0:
                    pe.wait_ge(s_wlo, 2 * IT * i + (j * IT + IT))
                if it == 0 and not (first and j == 0):
                    pe.wait_ge(s_acc, 2 * TG * TT * i + ((j - 1) * TG * TT + (g + 1) * TT))
                pe.wait_ge(s_hhi, n + 1)
                pe.wait_ge(s_hlo, n + 1)
                for t in range(TT):
                    for m, (ha, wa) in enumerate(((hid_hi, w_hi), (hid_hi, w_lo), (hid_lo, w_hi))):
                        mm = pe.matmul(ps[:, 4 + 2 * g + t // 2, t % 2 * H:(t % 2 + 1) * H], ha[:, par, t * P:(t + 1) * P],
                                       w2_of(wa, j, it), start=(it == 0 and m == 0 and t % 2 == 0),
                                       stop=(it == IT - 1 and m == 2), skip_group_check=True)
                    if final and t == TT // 2 - 1:
                        mm.then_inc(s_half_down, 1)
                mm.then_inc(s_down, 1)

            turn_xn(0)
            pe.wait_ge(s_xhi, HK)
            pe.wait_ge(s_xlo, HK)
            gate_up(0, 0, True)
            turn_y(1)
            gate_up(0, 1, True)

            def expert_pair(i, first, last):
                for v in range(UB):
                    if v + 2 < UB or not last:
                        gate_up(i, v + 2, first)
                    down(i, v, first, last and v == UB - 1)
                    if first and v == 0:
                        turn_xn(1)
                    if first and v == 1:
                        logits()
                    if first and v == 2:
                        turn_logits()
                    if first and v == 3:
                        pe.wait_ge(s_lga, 1)

            over_expert_pairs(pe, expert_pair)

        @block.vector
        def _(dve):
            dve.wait_ge(s_vec, 16)
            dve.tensor_scalar(half_conv_bias[:], conv_bias, 0.5, None, ALU.mult).then_inc(s_const_v, 1)
            dve.wait_ge(s_inw, 32)
            for et in range(ET):
                cols = slice(et * P, (et + 1) * P)
                dve.tensor_tensor(tapw[:, :, cols], convw[:, :, cols], inw[:, cols].unsqueeze(1).to_broadcast((P, TAPS, P)),
                                  ALU.mult).then_inc(s_tap, 1)

            def invert_variance(m, inv, steps, at):
                dve.wait_ge(steps, at)
                dve.tensor_scalar(m[:, :, 1], m[:, :, 1], EPS, None, ALU.add).then_inc(steps, 1)
                dve.wait_ge(steps, at + 1)
                dve.reciprocal(inv, m[:, :, 1]).then_inc(steps, 1)

            def refine_root(r, m, inv, steps, at, turn):
                dve.wait_ge(s_root, turn)
                dve.tensor_tensor(inv, r, r, ALU.mult).then_inc(steps, 1)
                dve.wait_ge(steps, at + 3)
                dve.tensor_tensor(inv, inv, m[:, :, 1], ALU.mult).then_inc(steps, 1)
                dve.wait_ge(steps, at + 4)
                dve.tensor_scalar(inv, inv, -0.5, 1.5, ALU.mult, ALU.add).then_inc(steps, 1)
                dve.wait_ge(steps, at + 5)
                dve.tensor_tensor(r, r, inv, ALU.mult).then_inc(steps, 1)
                dve.wait_ge(steps, at + RS)

            def make_u(n):
                dve.wait_ge(s_tanh, n + 1)
                dve.wait_ge(s_half, n + 1)
                dve.scalar_tensor_tensor(u[:, n], tanh_t[:, n], 1.0, half_t[:, n], ALU.add, ALU.mult).then_inc(s_u, 1)

            dve.wait_ge(s_x, 16 * TG)
            for t in range(NT):
                dve.bn_stats(stats[:, t], xs[:, t]).then_inc(s_ln1, 1)
            for t in range(NT):
                dve.wait_ge(s_ln1, t + 1)
                dve.bn_aggr(mv[:, t], stats[:, t]).then_inc(s_ln1, 1)
            make_u(0)
            invert_variance(mv, inv_var[:], s_ln1, 2 * NT)
            make_u(1)

            def first_root():
                refine_root(rstd[:], mv, inv_var[:], s_ln1, 2 * NT, 2)
                dve.tensor_scalar(half_rstd[:], rstd[:], 0.5, None, ALU.mult).then_inc(s_ln1, 1)
                dve.wait_ge(s_ln1, 2 * NT + RS + 1)
                dve.scalar_tensor_tensor(neg_half_mr[:], mv[:, :, 0], -1.0, half_rstd[:], ALU.mult, ALU.mult).then_inc(s_ln1, 1)

            dve.wait_ge(s_const, 4)
            for et in range(ET):
                dve.tensor_scalar(diag_d[:, et], ident[:], dskip[:, et:et + 1], None, ALU.mult).then_inc(s_const_v, 1)
            dve.wait_ge(s_alog, 1)
            dve.tensor_scalar(neg_a[:], exp_alog[:], -1.0, None, ALU.mult).then_inc(s_const_v, 1)

            def bc_left(p):
                dve.wait_ge(s_bca, p + 1)
                if p:
                    dve.wait_ge(s_bcv, 5 * p)
                dve.tensor_tensor(bc_rest[0:DT0, p], ps[0:DT0, x_proj_bank[p]], bc_round[0:DT0], ALU.subtract).then_inc(s_bcv, 1)

            def bc_parts(p):
                dve.tensor_copy(bc[0:BCR, p], bc_round[0:BCR]).then_inc(s_bcv, 1)
                dve.wait_ge(s_bcv, 5 * p + 1)
                dve.tensor_copy(bc_mid[2 * BCR:DT0], bc_rest[2 * BCR:DT0, p]).then_inc(s_bcv, 1)
                dve.tensor_copy(bc[BCR:2 * BCR, p], bc_rest[BCR:2 * BCR, p]).then_inc(s_bcv, 1)
                dve.wait_ge(s_bcv, 5 * p + 3)
                dve.tensor_tensor(bc[2 * BCR:DT0, p], bc_rest[2 * BCR:DT0, p], bc_mid[2 * BCR:DT0], ALU.subtract).then_inc(s_bcv, 1)

            def round_one_plus(p, et):
                dve.wait_ge(s_spa, 8 * p + 2 * ET + et + 1)
                dve.tensor_scalar(du[:, p * ET + et], sp_exp[p][:, et], 1.0, -1.0, ALU.add, ALU.add).then_inc(s_spv, 1)

            def delta_middle(p, et, at):
                n = p * ET + et
                dve.wait_ge(s_spv, at)
                dve.tensor_tensor(du[:, n], sp_exp[p][:, et], du[:, n], ALU.subtract).then_inc(s_spv, 1)
                dve.wait_ge(s_spv, at + 1)
                dve.tensor_tensor(du[:, n], sp_max[p][:, et], du[:, n], ALU.add).then_inc(s_spv, 1)

            def finish_delta(p, et, at):
                n = p * ET + et
                flat = delta[:, n].rearrange("p b l -> p (b l)")
                dve.wait_ge(s_spv, at)
                dve.wait_ge(s_spa, 8 * p + 3 * ET + et + 1)
                dve.tensor_tensor(flat, du[:, n], sp_ln[p][:, et], ALU.add).then_inc(s_spv, 1)
                dve.wait_ge(s_spv, at + 1)
                dve.tensor_tensor(du[:, n], flat, u[:, n], ALU.mult).then_inc(s_du, 1)

            def gated_z(p):
                for t in range(p * TT, (p + 1) * TT):
                    dve.wait_ge(s_zs, t + 1)
                    dve.scalar_tensor_tensor(zt[:, t], xs[:, t], mv[:, t, 0:1], zt[:, t], ALU.subtract, ALU.mult).then_inc(s_gz, 1)

            bc_left(0)
            bc_parts(0)
            for et in range(ET):
                round_one_plus(0, et)
                delta_middle(0, et, 3 * et + 1)
            for et in range(ET):
                finish_delta(0, et, 3 * ET + et)
            make_u(2)
            make_u(3)

            gz = zt[:].rearrange("p (q b k) l -> p q b k l", q=PAIRS, b=2)

            def gate_y(p):
                dve.wait_ge(s_gz, TT * (p + 1))
                for et in range(ET):
                    dve.wait_ge(s_sum, (p + 1) * N2 * ET)
                    dve.scalar_tensor_tensor(yg[:, p * ET + et], ps[:, et].rearrange("p (b l) -> p b l", b=2), 0.5,
                                             gz[:, p, :, et], ALU.mult, ALU.mult).then_inc(s_yg, 1)

            for p in range(PAIRS):
                dve.wait_ge(s_du, ET * (p + 1))
                def scans(i):
                    for par in range(2):
                        n2 = 2 * i + (p * N2 + par)
                        start = p == 0 and isinstance(i, int) and i == 0 and par == 0
                        dve.wait_ge(s_rows, n2 + 1)
                        for et in range(ET):
                            if not start:
                                dve.wait_ge(s_state, ET * n2 + et - (ET - 1))
                            dve.tensor_tensor(drive[:, et], du[:, p * ET + et].unsqueeze(1).to_broadcast((P, 2, T)),
                                              ps[:, 2 + 2 * par:4 + 2 * par], ALU.mult).then_inc(s_drive, 1)
                        if start:
                            bc_left(1)
                        for et in range(ET):
                            n = ET * n2 + et
                            dve.wait_ge(s_drive, n + 1)
                            dve.wait_ge(s_decay, 2 * n + 2)
                            if not (p == 0 and isinstance(i, int) and i == 0):
                                dve.wait_ge(s_prod, n - (2 * ET - 1))
                            dve.tensor_tensor_scan(states[par][et].rearrange("p j t -> p (j t)"),
                                                   decay[:, et].rearrange("p j b l -> p (j b l)"),
                                                   drive[:, et].rearrange("p j t -> p (j t)"),
                                                   0.0, ALU.mult, ALU.add).then_inc(s_state, 1)
                        if p and isinstance(i, int) and i == 0 and par == 0:
                            gate_y(p - 1)
                        first_of_all = p == 0 and isinstance(i, int) and i == 0
                        if first_of_all and par == 0:
                            bc_parts(1)
                            round_one_plus(1, 0)
                            first_root()
                        if first_of_all and par == 1:
                            round_one_plus(1, 1)
                            delta_middle(1, 1, 4 * ET + 2)
                            dve.wait_ge(s_spp, 2)
                            finish_delta(1, 0, 4 * ET + 4)
                        if p == 0 and isinstance(i, int) and i == N2 // 2 - 1 and par == 0:
                            dve.wait_ge(s_spp, 2)
                            finish_delta(1, 1, 4 * ET + 5)
                        if p == 0 and isinstance(i, int) and i == N2 // 2 - 1 and par == 1:
                            gated_z(0)
                over_state_pairs(dve, p, scans)

            def second_norm(g, between=None):
                tiles = slice(g * TT, (g + 1) * TT)
                at = (2 * TT + RS) * g
                dve.wait_ge(s_gz, TT * (g + 1))
                dve.wait_ge(s_zt, TT * (g + 1))
                for b in range(2):
                    first_tile = g * TT + 2 * b
                    dve.wait_ge(s_yt, 2 * g + b + 1)
                    x1 = xs[:, first_tile:first_tile + 2].rearrange("p t h -> p (t h)")
                    dve.tensor_tensor(x1, x1, ps[:, (2, 6)[g] + b], ALU.add).then_inc(s_x1, 1)
                for t in range(TT):
                    dve.wait_ge(s_x1, 2 * g + t // 2 + 1)
                    dve.bn_stats(stats2[:, g * TT + t], xs[:, g * TT + t]).then_inc(s_ln2, 1)
                for t in range(TT):
                    dve.wait_ge(s_ln2, at + t + 1)
                    dve.bn_aggr(mv2[:, g * TT + t], stats2[:, g * TT + t]).then_inc(s_ln2, 1)
                invert_variance(mv2[:, tiles], inv_var2[:, tiles], s_ln2, at + 2 * TT)
                if between:
                    between()
                refine_root(rstd2[:, tiles], mv2[:, tiles], inv_var2[:, tiles], s_ln2, at + 2 * TT, 3 + g)
                dve.wait_ge(s_state, PAIRS * N2 * ET)
                for t in range(g * TT, (g + 1) * TT):
                    dve.tensor_scalar(xn[:, t], xs[:, t], mv2[:, t, 0:1], rstd2[:, t:t + 1], ALU.subtract,
                                      ALU.mult).then_inc(s_xn, 1)

            def columns_low(g):
                for k in range(HK):
                    dve.wait_ge(s_xhi, HK * g + k + 1)
                    cols = slice(g * T, (g + 1) * T)
                    dve.tensor_tensor(xt_lo[:, k, cols], ps[:, 4 + HK * g + k], xt_hi[:, k, cols].bitcast(F32),
                                      ALU.subtract).then_inc(s_xlo, 1)

            over_e = lambda a: a.unsqueeze(2).to_broadcast((P, NT, E))
            steps = [0]

            def step(instruction):
                steps[0] += 1
                instruction.then_inc(s_rtv, 1)
                dve.wait_ge(s_rtv, steps[0])

            def router_probabilities():
                dve.wait_ge(s_lgl, 1)
                dve.tensor_tensor(lg_tanh[:], lg_tanh[:], lg_turned[:, :, 0:E], ALU.add).then_inc(s_lga, 1)
                dve.wait_ge(s_rta, 1)
                step(dve.tensor_reduce(lg_max[:], lg_tanh[:], AX_X, ALU.max))
                step(dve.tensor_tensor(lg_exp[:], lg_tanh[:], over_e(lg_max[:]), ALU.subtract))
                dve.wait_ge(s_rta, 2)
                step(dve.tensor_reduce(lg_sum[:], lg_exp[:], AX_X, ALU.add))
                step(dve.reciprocal(lg_sum[:], lg_sum[:]))
                dve.wait_ge(s_pad, 6)
                step(dve.tensor_tensor(probs[:, :, 0:E], lg_exp[:], over_e(lg_sum[:]), ALU.mult))

            def router_largest():
                for t in range(NT):
                    dve.max(top8[:, t], probs[:, t, 0:E]).then_inc(s_rtv, 1)
                steps[0] += NT
                dve.wait_ge(s_rtv, steps[0])
                step(dve.tensor_copy(chosen[:, :, 0:TOPK], top8[:, :, 0:TOPK]))

            def router_weights():
                for t in range(NT):
                    dve.match_replace(others[:, t], chosen[:, t], probs[:, t], 0.0).then_inc(s_rtv, 1)
                steps[0] += NT
                dve.wait_ge(s_rtv, steps[0])
                step(dve.tensor_tensor(weight[:], probs[:, :, 0:E], others[:, :, 0:E], ALU.subtract))

            second_norm(0)
            dve.wait_ge(s_small, 48)
            dve.wait_ge(s_wgz, 1)
            dve.tensor_copy(wg_parts[:, :, 0:E], wg[:]).then_inc(s_wg, 1)
            dve.wait_ge(s_wg, 1)
            dve.tensor_tensor(wg_parts[:, :, BCR:BCR + E], wg[:], wg_parts[:, :, 0:E].bitcast(F32), ALU.subtract).then_inc(s_wg, 1)
            columns_low(0)
            gated_z(1)
            gate_y(PAIRS - 1)

            weight_q = weight[:].rearrange("p t (i j) -> p t i j", j=2)

            def add_expert(i, j, g):
                final = isinstance(i, int) and i == E // 2 - 1 and j == 1 and g == TG - 1
                if final:
                    dve.wait_ge(s_half_down, 1)
                else:
                    dve.wait_ge(s_down, UB * i + (j * UE + (g + 1) * IT))
                for t in range(TT):
                    if final and t == TT // 2:
                        dve.wait_ge(s_down, UB * E // 2)
                    a = g * TT + t
                    dve.scalar_tensor_tensor(xs[:, a], ps[:, 4 + 2 * g + t // 2, t % 2 * H:(t % 2 + 1) * H],
                                             weight_q[:, a, i, j:j + 1], xs[:, a], ALU.mult, ALU.add).then_inc(s_acc, 1)

            def hidden(i, v, first):
                n = UB * i + v
                dve.wait_ge(s_gt, n + 1)
                if not first or v >= 2:
                    dve.wait_ge(s_hid, n - 1)
                dve.scalar_tensor_tensor(g_silu2[:, v % 2], g_tanh[:, v % 2], 1.0, ps[:, gate_bank(v)], ALU.add,
                                         ALU.mult).then_inc(s_gs, 1)
                dve.wait_ge(s_gs, n + 1)
                dve.wait_ge(s_up, n + 1)
                if not first or v >= 2:
                    dve.wait_ge(s_hlo, n - 1)
                dve.scalar_tensor_tensor(hid[:, v % 2], g_silu2[:, v % 2], 0.5, ps[:, gate_bank(v) + 1], ALU.mult,
                                         ALU.mult).then_inc(s_hid, 1)

            def expert_pair(i, first, last):
                for v in range(UB):
                    if first and v == 1:
                        continue
                    hidden(i, v, first)
                    if first and v == 0:
                        second_norm(1, lambda: hidden(i, 1, first))
                    if first and v == 2:
                        columns_low(1)
                    if first and 3 <= v < 6:
                        (router_probabilities, router_largest, router_weights)[v - 3]()
                    if v == 2 and not first:
                        add_expert(i - 1, 1, TG - 1)
                    if v in (6, 10, 14):
                        add_expert(i, (v - 3) // UE, (v - 3) // IT % TG)

            over_expert_pairs(dve, expert_pair)
            add_expert(E // 2 - 1, 1, TG - 1)


def kernel(x, ctx_1024, L0_xattn_in_proj_w, L0_xattn_conv_w, L0_xattn_conv_b, L0_xattn_x_proj_w, L0_xattn_dt_proj_w,
           L0_xattn_dt_proj_b, L0_xattn_A_log, L0_xattn_D, L0_ffn_w_gate, L0_ffn_w1, L0_ffn_w3, L0_ffn_w2):
    import numpy as np
    import concourse.bacc as bacc
    from concourse.bass_utils import run_bass_kernel_spmd

    x_proj_t = np.transpose(L0_xattn_x_proj_w)
    dt_rank = L0_xattn_dt_proj_w.shape[1]
    given = {
        "x": x, "ctx_t": np.transpose(ctx_1024, (2, 0, 1)), "in_proj_t": np.transpose(L0_xattn_in_proj_w),
        "conv_w_t": np.transpose(L0_xattn_conv_w),
        "channel_rows": np.concatenate([L0_xattn_conv_b[:, None], L0_xattn_dt_proj_b[:, None],
                                        L0_xattn_D[:, None], L0_xattn_A_log], axis=1),
        "x_proj_rows": np.concatenate([x_proj_t[:, dt_rank:]] * 3 + [x_proj_t[:, :dt_rank]], axis=1),
        "dt_proj_t": np.transpose(L0_xattn_dt_proj_w),
        "w_gate": L0_ffn_w_gate, "w1": L0_ffn_w1, "w3": L0_ffn_w3, "w2": L0_ffn_w2,
    }
    nc = bacc.Bacc("TRN2", target_bir_lowering=False, num_devices=1)
    arrays, args = {}, {}
    for name, a in given.items():
        a = np.ascontiguousarray(a)
        arrays[f"in_{name}"] = a
        args[name] = nc.dram_tensor(f"in_{name}", a.shape, mybir.dt.from_np(a.dtype), kind="ExternalInput").ap()
    out = nc.dram_tensor("out", x.shape, F32, kind="ExternalOutput").ap()
    xattn_ffn(nc, **args, out=out)
    r = run_bass_kernel_spmd(nc, [arrays], core_ids=[0])
    return r.results[0]["out"]
```
